# Optimizing a Trainium2 kernel written in Bass

```python
import numpy as np
import jax
import jax.numpy as jnp

def _softmax(x, axis=-1):
    return jax.nn.softmax(x, axis=axis)

def _gelu(x):
    return jax.nn.gelu(x, approximate=True)

def _silu(x):
    return jax.nn.silu(x)

def _sigmoid(x):
    return jax.nn.sigmoid(x)

def _layernorm(x, axis=-1, eps=1e-05):
    m = jnp.mean(x, axis=axis, keepdims=True)
    v = jnp.var(x, axis=axis, keepdims=True)
    return (x - m) / jnp.sqrt(v + eps)

def _scatter_add(tgt, idx, src, axis=0):
    return tgt.at[idx].add(src)

def _segment_sum(src, seg, n):
    return jax.ops.segment_sum(src, seg, n)
kernel_name = 'mk_flamingo_gated_d1_seqx_r4_53f67a'

def setup_inputs(seed: int=0):
    np.random.seed(seed)
    _w = jnp.asarray

    def _rec_inputs():
        import jax
        import jax.numpy as jnp
        _rk = jax.random.key(seed)
        x = -0.000125 + 0.9999 * jax.random.normal(jax.random.fold_in(_rk, 1), (4, 512, 512), jnp.float32)
        _lenS = 512 - jax.random.randint(jax.random.fold_in(_rk, 7), (4,), 0, max(1, 512 // 4) + 1, jnp.int32)
        _lenS2 = 512 - jax.random.randint(jax.random.fold_in(_rk, 8), (4,), 0, max(1, 512 // 4) + 1, jnp.int32)
        itok_BxS_13_99985 = jax.random.randint(jax.random.fold_in(_rk, 11), (4, 512), 13, 99986, jnp.int32)
        _ctx_2048P = jax.random.normal(jax.random.fold_in(_rk, 12), (4, 16, 512), jnp.float32)
        _ctx_2048c = jax.random.dirichlet(jax.random.fold_in(_rk, 512), 0.3 * jnp.ones((16,), jnp.float32), (4, 512))
        _ctx_2048t = jnp.einsum('bsk,bkd->bsd', _ctx_2048c, _ctx_2048P)
        _ctx_2048t = _ctx_2048t * jax.lax.rsqrt(jnp.mean(jnp.square(_ctx_2048t)) + 1e-12) * 0.953939
        ctx_2048 = 6.82029e-06 + 0.0200006 * (_ctx_2048t + 0.3 * jax.random.normal(jax.random.fold_in(_rk, 612), (4, 512, 512), jnp.float32))
        _g = jax.random.normal(jax.random.fold_in(_rk, 9001), (2, 1), jnp.float32)
        _g = jnp.sign(_g) * jnp.maximum(jnp.abs(_g), 1.0) + (_g == 0) * 1.0
        g_xattn = _g[0]
        g_ffn = _g[1]
        return (x, itok_BxS_13_99985, ctx_2048, g_xattn, g_ffn)
    x, itok_BxS_13_99985, ctx_2048, g_xattn, g_ffn = _rec_inputs()

    def _L0_xattn_setup():
        import jax, jax.numpy as jnp
        import numpy as np
        B, S, D = (4, 1024, 512)
        E = 4
        F = 2048 // E
        VOCAB = 25000
        key = jax.random.key(seed)
        k1, k2, k3, k4, k5 = jax.random.split(key, 5)
        hidden_states = jax.random.normal(k1, (B, S, D), dtype=jnp.float32)
        token_ids = jax.random.randint(k2, (B, S), 0, VOCAB, dtype=jnp.int64)
        Wg = jax.random.normal(k3, (E, F, D), dtype=jnp.float32) * 0.02
        Wu = jax.random.normal(k4, (E, F, D), dtype=jnp.float32) * 0.02
        Wd = jax.random.normal(k5, (E, D, F), dtype=jnp.float32) * 0.02
        return {'hidden_states': hidden_states, 'token_ids': token_ids, 'Wg': Wg, 'Wu': Wu, 'Wd': Wd}
    _L0_xattn_all = _L0_xattn_setup()
    _L0_xattn_in = {k: v for k, v in _L0_xattn_all.items() if k in ()}
    del _L0_xattn_all

    def _L0_ffn_setup():
        import jax, jax.numpy as jnp
        import numpy as np
        D = 512
        E = 8
        R = 16
        K = 2
        INIT_BONUS = 3.0
        ANNEAL_STEPS = 1250
        CURRENT_STEP = 1
        key = jax.random.key(seed)
        ks = jax.random.split(key, 7)
        s_in = 1.0 / np.sqrt(D)
        s_r = 1.0 / np.sqrt(R)
        return {'x': jax.random.normal(ks[0], (2, 1024, D), dtype=jnp.float32), 'Wr': jax.random.normal(ks[1], (D, E), dtype=jnp.float32) * s_in, 'br': jax.random.normal(ks[2], (E,), dtype=jnp.float32) * 0.01, 'Wd': jax.random.normal(ks[3], (E, D, R), dtype=jnp.float32) * s_in, 'bd': jnp.zeros((E, R), dtype=jnp.float32), 'Wu': jax.random.normal(ks[4], (E, R, D), dtype=jnp.float32) * s_r, 'bu': jnp.zeros((E, D), dtype=jnp.float32)}
    _L0_ffn_all = _L0_ffn_setup()
    _L0_ffn_in = {k: v for k, v in _L0_ffn_all.items() if k in ('Wr', 'br', 'Wd', 'bd', 'Wu', 'bu')}
    del _L0_ffn_all
    return {'x': x, 'itok_BxS_13_99985': itok_BxS_13_99985, 'ctx_2048': ctx_2048, 'g_xattn': g_xattn, 'g_ffn': g_ffn, 'L0_ffn_Wr': _L0_ffn_in['Wr'], 'L0_ffn_br': _L0_ffn_in['br'], 'L0_ffn_Wd': _L0_ffn_in['Wd'], 'L0_ffn_bd': _L0_ffn_in['bd'], 'L0_ffn_Wu': _L0_ffn_in['Wu'], 'L0_ffn_bu': _L0_ffn_in['bu']}

def reference(x, itok_BxS_13_99985, ctx_2048, g_xattn, g_ffn, L0_ffn_Wr, L0_ffn_br, L0_ffn_Wd, L0_ffn_bd, L0_ffn_Wu, L0_ffn_bu):
    import jax
    import jax.numpy as jnp

    def _L0_xattn_ref(hidden_states, token_ids, Wg, Wu, Wd):
        import jax, jax.numpy as jnp
        import numpy as np
        B, S, D = (4, 1024, 512)
        E = 4
        F = 2048 // E
        VOCAB = 25000
        tokens_per_expert = VOCAB // E
        tid = jnp.clip(token_ids, 0, VOCAB - 1)
        expert_ids = jnp.minimum(tid // tokens_per_expert, E - 1)
        out = jnp.zeros_like(hidden_states)
        for e in range(E):
            g = jax.nn.silu(jnp.einsum('bsd,fd->bsf', hidden_states, Wg[e]))
            u = jnp.einsum('bsd,fd->bsf', hidden_states, Wu[e])
            y = jnp.einsum('bsf,df->bsd', g * u, Wd[e])
            out = jnp.where((expert_ids == e)[..., None], y, out)
        return out

    def _L0_ffn_ref(x, Wr, br, Wd, bd, Wu, bu):
        import jax, jax.numpy as jnp
        import numpy as np
        D = 512
        E = 8
        R = 16
        K = 2
        INIT_BONUS = 3.0
        ANNEAL_STEPS = 1250
        CURRENT_STEP = 1
        logits = jnp.einsum('btd,de->bte', x, Wr) + br
        progress = min(CURRENT_STEP / ANNEAL_STEPS, 1.0)
        bonus = INIT_BONUS * (1.0 - progress)
        logits = logits + bonus
        gates = jax.nn.softmax(logits, axis=-1)
        topk_vals, topk_idx = jax.lax.top_k(gates, K)
        topk_vals = topk_vals / topk_vals.sum(axis=-1, keepdims=True)
        w = (jax.nn.one_hot(topk_idx, E, dtype=x.dtype) * topk_vals[..., None]).sum(axis=-2)
        h = jax.nn.relu(jnp.einsum('btd,edr->betr', x, Wd) + bd[None, :, None, :])
        eo = jnp.einsum('betr,erd->betd', h, Wu) + bu[None, :, None, :]
        out = jnp.einsum('bte,betd->btd', w, eo)
        return out
    x = x + jnp.tanh(g_xattn[0]) * _L0_xattn_ref(_layernorm(x, axis=-1), itok_BxS_13_99985, ctx_2048, ctx_2048, ctx_2048)
    x = x + jnp.tanh(g_ffn[0]) * _L0_ffn_ref(_layernorm(x, axis=-1), L0_ffn_Wr, L0_ffn_br, L0_ffn_Wd, L0_ffn_bd, L0_ffn_Wu, L0_ffn_bu)
    return x

_drawn_inputs = setup_inputs


def setup_inputs(seed=0):
    import zlib

    import numpy as np

    out = dict(_drawn_inputs(seed))
    spreads = {'L0_ffn_bd': (0.0, 0.1), 'L0_ffn_bu': (0.0, 0.1)}
    factors = {}
    for name, (base, spread) in spreads.items():
        noise = np.random.default_rng([zlib.crc32(name.encode()), seed]).standard_normal(out[name].shape)
        drawn = base * np.exp(spread * noise) if base else spread * noise
        out[name] = jnp.asarray(drawn.astype(out[name].dtype))
    for name, factor in factors.items():
        out[name] = (out[name] * factor).astype(out[name].dtype)
    return out
```

```python
import numpy as np
import concourse.bass as bass
from concourse import mybir
from contextlib import ExitStack


def bass_flamingo_gated_kernel(
    nc: bass.Bass,
    x: bass.AP,
    tok: bass.AP,
    ctx_w: bass.AP,
    g_xattn: bass.AP,
    g_ffn: bass.AP,
    Wr: bass.AP,
    br: bass.AP,
    Wd: bass.AP,
    bd: bass.AP,
    Wu: bass.AP,
    bu: bass.AP,
    out: bass.AP,
):
    fp32, fp16 = mybir.dt.float32, mybir.dt.float16
    i32, u32 = mybir.dt.int32, mybir.dt.uint32
    ALU = mybir.AluOpType
    ACT = mybir.ActivationFunctionType
    AX = mybir.AxisListType

    P = 128
    B, S, D = x.shape
    N = B * S
    E = ctx_w.shape[0]
    KC = D // P
    C = N // P
    T = N // P + E - 1
    VOCAB = 25000
    PER_EXPERT = VOCAB // E
    EF, _, R = Wd.shape
    ER = EF * R
    HC = ER + EF
    BONUS = 3.0 * (1.0 - min(1 / 1250, 1.0))
    EPS = 1e-5
    SKIP = 2 * N

    WK = 10
    PK = 15
    SB = 127 + 63 + WK
    ONE_EXP = float(1 << 23)

    x_rows = x.rearrange("b s d -> (b s) d")
    out_rows = out.rearrange("b s d -> (b s) d")

    ctx = ExitStack()
    with ctx:
        def sb(name, shape, dt=fp32):
            return ctx.enter_context(nc.sbuf_tensor(name, shape, dt))

        def pb(name, shape, dt=fp32):
            return ctx.enter_context(nc.psum_tensor(name, shape, dt))

        def sem(name):
            return ctx.enter_context(nc.semaphore(name))

        ident = sb("ident", [P, P])
        before = sb("before", [P, P])
        ones = sb("ones", [P, P])
        slot_no = sb("slot_no", [P, P])
        tile_no = sb("tile_no", [P, T])
        count_edge = sb("count_edge", [P, C])
        row_id1 = sb("row_id1", [P, C])

        tok_i = sb("tok_i", [P, C], i32)
        ge = sb("ge", [P, E + 1, C])
        member = sb("member", [P, E, C])
        zeros = sb("zeros", [P, E * C])
        run = sb("run", [P, E * C])
        per_row = sb("per_row", [P, E])
        prev_end = sb("prev_end", [P, E])
        over = sb("over", [P, E, C])
        tiles_of = sb("tiles_of", [P, E])
        tile_end = sb("tile_end", [P, E])
        first_slot = sb("first_slot", [P, E])
        shift = sb("shift", [P, E])
        cand = sb("cand", [P, E, C])
        slot1 = sb("slot1", [P, C])
        slot_i = sb("slot_i", [P, C], i32)
        tile_i = sb("tile_i", [P, C], i32)
        in_tile_i = sb("in_tile_i", [P, C], i32)
        tile_f = sb("tile_f", [P, C])
        in_tile_f = sb("in_tile_f", [P, C])
        hot_slot = sb("hot_slot", [P, C, P], fp16)
        hot_tile = sb("hot_tile", [P, C, T], fp16)
        is_tile = sb("is_tile", [P, C, T])
        row1 = sb("row1", [P, T])
        pad = sb("pad", [P, T])
        gather_rows = sb("gather_rows", [P, T], u32)
        scatter_f = sb("scatter_f", [P, T])
        scatter_rows = sb("scatter_rows", [P, T], u32)
        past = sb("past", [P, E - 1, T])
        expert_f = sb("expert_f", [P, T])
        expert_i = sb("expert_i", [P, T], i32)

        w_nat = sb("w_nat", [P, E, KC, D])
        w_hi = sb("w_hi", [P, E, KC, D], fp16)
        w_lo = sb("w_lo", [P, E, KC, D], fp16)
        sq = sb("sq", [P, D])
        row_sq = sb("row_sq", [P, E * KC])
        part_sq = sb("part_sq", [P, 1])
        top_sq = sb("top_sq", [1, 1])
        top_all = sb("top_all", [P, 1])
        half_exp = sb("half_exp", [P, 1], i32)
        scale_w = sb("scale_w", [P, 1], i32)
        scale_inv = sb("scale_inv", [P, 1], i32)
        s_w = scale_w[:, :].bitcast(fp32)
        s_inv = scale_inv[:, :].bitcast(fp32)
        p_coef = sb("p_coef", [P, 1])
        inv2 = sb("inv2", [P, 1])
        inv3 = sb("inv3", [P, 1])
        y_coef = sb("y_coef", [P, 1])
        gates_in = sb("gates_in", [P, 2])
        gates = sb("gates", [P, 2])

        wd_nat = sb("wd_nat", [P, EF, KC, R])
        wr_nat = sb("wr_nat", [P, KC, EF])
        w_in = sb("w_in", [P, KC, HC])
        b_in = sb("b_in", [P, HC])
        wu_sb = sb("wu_sb", [ER, D])
        bu_sb = sb("bu_sb", [EF, D])

        xs = sb("xs", [P, T, D])
        st1 = sb("st1", [P, 6])
        mv1 = sb("mv1", [P, 2])
        st2 = sb("st2", [P, 6])
        mv2 = sb("mv2", [P, 2])
        ve = sb("ve", [P, 2, T])
        rs = sb("rs", [P, 2, T])
        mrs = sb("mrs", [P, 2, T])
        neg_half = sb("neg_half", [P, 1])
        neg_one = sb("neg_one", [P, 1])
        h = sb("h", [P, D])
        hT_hi = sb("hT_hi", [P, KC, P], fp16)
        hT_lo = sb("hT_lo", [P, KC, P], fp16)
        silu = sb("silu", [P, D])
        prod = sb("prod", [P, D])
        pT_hi = sb("pT_hi", [P, KC, P], fp16)
        pT_lo = sb("pT_lo", [P, KC, P], fp16)
        h2 = sb("h2", [P, KC, P])
        h2T = sb("h2T", [P, KC, P])
        hid = sb("hid", [P, HC])
        top8 = sb("top8", [P, 8])
        arg8 = sb("arg8", [P, 8], u32)
        arg8f = sb("arg8f", [P, 8])
        gate_cell = sb("gate_cell", [P, 5])
        gap = sb("gap", [P, 1])
        half_tanh = sb("half_tanh", [P, 1])
        w_top = sb("w_top", [P, 2])
        w_first = sb("w_first", [P, EF])
        w_second = sb("w_second", [P, EF])
        weighted = sb("weighted", [P, HC])
        wtT = sb("wtT", [P, P])
        gwT = sb("gwT", [EF, P])

        ps_hT = pb("ps_hT", [P, KC, P])
        ps_a = pb("ps_a", [P, D])
        ps_pT = pb("ps_pT", [P, KC, P])
        ps_y = pb("ps_y", [P, D])
        ps_h2T = pb("ps_h2T", [P, KC, P])
        ps_hid = pb("ps_hid", [P, D])
        ps_wT = pb("ps_wT", [P, KC, P])
        ps_o = pb("ps_o", [P, D])

        s_tok = sem("s_tok")
        s_wload = [sem(f"s_wload{e}") for e in range(E)]
        s_small = sem("s_small")
        s_gather = [sem(f"s_gather{t}") for t in range(T)]
        s_scatter = sem("s_scatter")
        s_const = sem("s_const")
        s_pool = sem("s_pool")
        s_route = sem("s_route")
        s_counts = sem("s_counts")
        s_rows_mm = sem("s_rows_mm")
        s_hot = sem("s_hot")
        s_gather_rows = sem("s_gather_rows")
        s_scatter_rows = sem("s_scatter_rows")
        s_expert = sem("s_expert")
        s_rowsq = sem("s_rowsq")
        s_sq = sem("s_sq")
        s_partsq = sem("s_partsq")
        s_sqT = sem("s_sqT")
        s_topsq = sem("s_topsq")
        s_topall = sem("s_topall")
        s_scale = sem("s_scale")
        s_gates = sem("s_gates")
        s_coef = sem("s_coef")
        s_wT = sem("s_wT")
        s_whi = sem("s_whi")
        s_wlo = sem("s_wlo")
        s_ffn_w = sem("s_ffn_w")
        x_in = sem("x_in")
        stats1 = sem("stats1")
        aggr1 = sem("aggr1")
        rstd1 = sem("rstd1")
        normed1 = sem("normed1")
        hT_done = sem("hT_done")
        hT_hi_done = sem("hT_hi_done")
        hT_lo_done = sem("hT_lo_done")
        a_done = sem("a_done")
        silu_done = sem("silu_done")
        prod_done = sem("prod_done")
        pT_done = sem("pT_done")
        pT_hi_done = sem("pT_hi_done")
        pT_lo_done = sem("pT_lo_done")
        y_done = sem("y_done")
        x1_done = sem("x1_done")
        stats2 = sem("stats2")
        aggr2 = sem("aggr2")
        rstd2 = sem("rstd2")
        rs_step = sem("rs_step")
        normed2 = sem("normed2")
        h2T_done = sem("h2T_done")
        h2T_copied = sem("h2T_copied")
        hid_mm = sem("hid_mm")
        hid_done = sem("hid_done")
        top_done = sem("top_done")
        arg_done = sem("arg_done")
        argf_done = sem("argf_done")
        gap_done = sem("gap_done")
        tanh_done = sem("tanh_done")
        wtop_done = sem("wtop_done")
        wfirst_done = sem("wfirst_done")
        wsecond_done = sem("wsecond_done")
        gate_w_done = sem("gate_w_done")
        weighted_done = sem("weighted_done")
        wtT_done = sem("wtT_done")
        wtT_copied = sem("wtT_copied")
        o_mm = sem("o_mm")
        out_done = sem("out_done")

        block = ctx.enter_context(nc.Block())

        FULL0, FULL1 = 3, T - 3
        FIRST, LAST = -3, T + 3

        def pipeline(eng, step):
            for i in range(FIRST, FULL0):
                step(i, lambda k: 0 <= k < T)
            with eng.Fori(FULL0, FULL1) as i:
                step(i, lambda k: True)
            for i in range(FULL1, LAST):
                step(i, lambda k: 0 <= k < T)

        def col(k):
            return bass.ds(k, 1)

        def wait_last(eng, done, k):
            if not (isinstance(k, int) and k == 0):
                eng.wait_ge(done, k)

        @block.sync
        def _(sp):
            sp.dma_start(tok_i[:, :], tok.rearrange("b (q c) -> (b q) c", c=C)).then_inc(s_tok, 16)
            for e in range(E):
                sp.dma_start(w_nat[:, e, :, :], ctx_w[e, :, :].rearrange("(c p) k -> p c k", p=P))\
                  .then_inc(s_wload[e], 16)
            for t in range(T):
                sp.wait_ge(s_gather[t], 16)
                sp.sem_inc(x_in, 1)
            sp.wait_ge(s_scatter, 16 * T)

        @block.gpsimd
        def _(pool):
            g = nc.gpsimd
            g.memset(ident[:, :], 0.0).then_inc(s_pool, 1)
            g.memset(before[:, :], 1.0).then_inc(s_pool, 1)
            g.memset(ones[:, :], 1.0)
            g.memset(neg_half[:, :], -0.5)
            g.memset(neg_one[:, :], -1.0)
            g.iota(count_edge[:, :], pattern=[[P, C]], base=0, channel_multiplier=0,
                   allow_small_or_imprecise_dtypes=True)
            pool.wait_ge(s_pool, 2)
            g.affine_select(out=ident[:, :], in_=ident[:, :], compare_op=ALU.not_equal, fill=1.0,
                            base=0, pattern=[[-1, P]], channel_multiplier=1)
            g.affine_select(out=before[:, :], in_=before[:, :], compare_op=ALU.is_gt, fill=0.0,
                            base=0, pattern=[[1, P]], channel_multiplier=-1)
            g.iota(row_id1[:, :], pattern=[[1, C]], base=1, channel_multiplier=C,
                   allow_small_or_imprecise_dtypes=True)
            g.iota(tile_no[:, :], pattern=[[1, T]], base=0, channel_multiplier=0,
                   allow_small_or_imprecise_dtypes=True)
            g.iota(slot_no[:, :], pattern=[[1, P]], base=0, channel_multiplier=0,
                   allow_small_or_imprecise_dtypes=True).then_inc(s_const, 1)
            pool.wait_ge(s_gather_rows, 1)
            for t in range(T):
                g.indirect_dma_start(
                    out=xs[:, t, :], out_offset=None, in_=x_rows[:, :],
                    in_offset=bass.IndirectOffsetOnAxis(ap=gather_rows[:, t:t + 1], axis=0),
                ).then_inc(s_gather[t], 16)
            steps = [0]

            def step(ins):
                steps[0] += 1
                ins.then_inc(rs_step, 1)
                pool.wait_ge(rs_step, steps[0])

            def rstd(n, mv, k, done):
                step(g.tensor_scalar(ve[:, n, k:k + 1], mv[:, 1:2], EPS, None, ALU.add))
                step(g.tensor_tensor(rs[:, n, k:k + 1], ve[:, n, k:k + 1], neg_half[:, :], ALU.pow))
                step(g.tensor_tensor(ve[:, n, k:k + 1], mv[:, 0:1], neg_one[:, :], ALU.mult))
                g.tensor_tensor(mrs[:, n, k:k + 1], ve[:, n, k:k + 1], rs[:, n, k:k + 1],
                                ALU.mult).then_inc(done, 1)

            for i in range(FIRST, LAST):
                if 0 <= i + 3 < T:
                    pool.wait_ge(aggr1, i + 4)
                    rstd(0, mv1, i + 3, rstd1)
                if 0 <= i - 1 < T:
                    pool.wait_ge(aggr2, i)
                    rstd(1, mv2, i - 1, rstd2)
                if i == 0:
                    pool.wait_ge(s_scatter_rows, 1)
                if 0 <= i - 3 < T:
                    pool.wait_ge(out_done, i - 2)
                    g.indirect_dma_start(
                        out=out_rows[:, :],
                        out_offset=bass.IndirectOffsetOnAxis(ap=scatter_rows[:, i - 3:i - 2], axis=0),
                        in_=xs[:, i - 3, :], in_offset=None,
                        bounds_check=N - 1, oob_is_err=False,
                    ).then_inc(s_scatter, 16)

        @block.tensor
        def _(pe):
            mm, tr = nc.tensor.matmul, nc.tensor.transpose
            pe.wait_ge(s_const, 1)
            pe.wait_ge(s_counts, 1)
            mm(ps_a[:, 0:E], before[:, :], per_row[:, :], start=True, stop=True)
            mm(ps_y[:, 0:E], ones[:, :], per_row[:, :], start=True, stop=True).then_inc(s_rows_mm, 1)
            pe.wait_ge(s_hot, 1)
            for c in range(C):
                last = mm(ps_pT[:, 0, 0:T], hot_slot[:, c, :], hot_tile[:, c, :],
                          start=(c == 0), stop=(c == C - 1))
            last.then_inc(s_rows_mm, 1)
            pe.wait_ge(s_partsq, 1)
            tr(ps_h2T[0:1, 0, :], part_sq[:, :], ident[:, :]).then_inc(s_sqT, 1)
            pe.wait_ge(s_topsq, 1)
            mm(ps_o[:, 0:1], ones[0:1, :], top_sq[:, :], start=True, stop=True).then_inc(s_topall, 1)
            banks = [ps_hT, ps_wT]
            for n in range(E * KC):
                e, kc = n // KC, n % KC
                if n >= 2:
                    pe.wait_ge(s_wlo, n - 1)
                if kc == 0:
                    pe.wait_ge(s_wload[e], 16)
                for c in range(KC):
                    last = tr(banks[n % 2][:, c, :], w_nat[:, e, c, kc * P:(kc + 1) * P], ident[:, :])
                last.then_inc(s_wT, 1)
            pe.wait_ge(s_wlo, E * KC)
            pe.wait_ge(s_ffn_w, 1)
            pe.wait_ge(s_expert, 1)

            def split_product(ps, lhs_hi, lhs_lo, e):
                for kc in range(KC):
                    hi = w_hi[:, bass.ds(e, 1), kc, :].rearrange("p e n -> p (e n)")
                    lo = w_lo[:, bass.ds(e, 1), kc, :].rearrange("p e n -> p (e n)")
                    mm(ps[:, :], lhs_hi[:, kc, :], hi, start=(kc == 0), stop=False)
                    mm(ps[:, :], lhs_hi[:, kc, :], lo, start=False, stop=False)
                    last = mm(ps[:, :], lhs_lo[:, kc, :], hi, start=False, stop=(kc == KC - 1))
                return last

            def step(i, has):
                if has(i - 1):
                    k = i - 1
                    pe.wait_ge(prod_done, k + 1)
                    for c in range(KC):
                        last = tr(ps_pT[:, c, :], prod[:, c * P:(c + 1) * P], ident[:, :])
                    last.then_inc(pT_done, 1)
                if has(i):
                    k = i
                    e = pe.value_load(expert_i[0:1, col(k)], min_val=0, max_val=E - 1)
                    pe.wait_ge(hT_lo_done, k + 1)
                    split_product(ps_a, hT_hi, hT_lo, e).then_inc(a_done, 1)
                if has(i - 2):
                    k = i - 2
                    pe.wait_ge(normed2, k + 1)
                    for c in range(KC):
                        last = tr(ps_h2T[:, c, :], h2[:, c, :], ident[:, :])
                    last.then_inc(h2T_done, 1)
                if has(i - 3):
                    k = i - 3
                    pe.wait_ge(weighted_done, k + 1)
                    tr(ps_wT[:, 0, :], weighted[:, 0:ER], ident[:, :])
                    tr(ps_wT[0:EF, 1, :], weighted[:, ER:HC], ident[:, :]).then_inc(wtT_done, 1)
                if has(i + 1):
                    k = i + 1
                    pe.wait_ge(normed1, k + 1)
                    for c in range(KC):
                        last = tr(ps_hT[:, c, :], h[:, c * P:(c + 1) * P], ident[:, :])
                    last.then_inc(hT_done, 1)
                if has(i - 1):
                    k = i - 1
                    e = pe.value_load(expert_i[0:1, col(k)], min_val=0, max_val=E - 1)
                    pe.wait_ge(pT_lo_done, k + 1)
                    wait_last(pe, x1_done, k)
                    split_product(ps_y, pT_hi, pT_lo, e).then_inc(y_done, 1)
                if has(i - 2):
                    k = i - 2
                    pe.wait_ge(h2T_copied, k + 1)
                    for c in range(KC):
                        last = mm(ps_hid[:, 0:HC], h2T[:, c, :], w_in[:, c, :],
                                  start=(c == 0), stop=(c == KC - 1))
                    last.then_inc(hid_mm, 1)
                if has(i - 3):
                    k = i - 3
                    pe.wait_ge(wtT_copied, k + 1)
                    wait_last(pe, out_done, k)
                    mm(ps_o[:, :], wtT[:, :], wu_sb[:, :], start=True, stop=False)
                    mm(ps_o[:, :], gwT[:, :], bu_sb[:, :], start=False, stop=True).then_inc(o_mm, 1)

            pipeline(pe, step)

        @block.scalar
        def _(act):
            a = nc.scalar.activation
            act.dma_start(gates_in[:, 0:1], g_xattn.rearrange("(a n) -> a n", a=1).to_broadcast([P, 1])).then_inc(s_small, 16)
            act.dma_start(gates_in[:, 1:2], g_ffn.rearrange("(a n) -> a n", a=1).to_broadcast([P, 1])).then_inc(s_small, 16)
            act.dma_start(b_in[:, 0:ER], bd.rearrange("(a e) r -> a (e r)", a=1).to_broadcast([P, ER])).then_inc(s_small, 16)
            act.dma_start(b_in[:, ER:HC], br.rearrange("(a e) -> a e", a=1).to_broadcast([P, EF])).then_inc(s_small, 16)
            act.dma_start(wr_nat[:, :, :], Wr.rearrange("(p c) e -> p c e", c=KC)).then_inc(s_small, 16)
            act.dma_start(wd_nat[:, :, :, :], Wd.rearrange("e (p c) r -> p e (c r)", c=KC)).then_inc(s_small, 16)
            act.dma_start(wu_sb[:, :], Wu.rearrange("e r d -> (e r) d")).then_inc(s_small, 16)
            act.dma_start(bu_sb[:, :], bu[:, :]).then_inc(s_small, 16)
            for n in range(E * KC):
                if n % KC == 0:
                    act.wait_ge(s_wload[n // KC], 16)
                if n:
                    act.wait_ge(s_sq, n)
                a(sq[:, :], w_nat[:, n // KC, n % KC, :], ACT.Square,
                  accum_out=row_sq[:, n:n + 1]).then_inc(s_sq, 1)
            act.wait_ge(s_small, 16 * 8)
            a(gates[:, :], gates_in[:, :], ACT.Tanh).then_inc(s_gates, 1)
            banks = [ps_hT, ps_wT]
            act.wait_ge(s_scale, 1)
            for n in range(E * KC):
                act.wait_ge(s_wT, n + 1)
                a(w_hi[:, n // KC, n % KC, :], banks[n % 2][:, :, :].rearrange("p c q -> p (c q)"),
                  ACT.Copy, scale=s_w).then_inc(s_whi, 1)

            def step(i, has):
                if has(i - 1):
                    k = i - 1
                    act.wait_ge(pT_done, k + 1)
                    wait_last(act, y_done, k)
                    a(pT_hi[:, :, :], ps_pT[:, :, :], ACT.Copy).then_inc(pT_hi_done, 1)
                if has(i):
                    k = i
                    act.wait_ge(a_done, k + 1)
                    a(silu[:, :], ps_a[:, :], ACT.Silu, scale=s_inv).then_inc(silu_done, 1)
                if has(i - 2):
                    k = i - 2
                    act.wait_ge(h2T_done, k + 1)
                    wait_last(act, hid_mm, k)
                    a(h2T[:, :, :], ps_h2T[:, :, :], ACT.Copy).then_inc(h2T_copied, 1)
                if has(i - 3):
                    k = i - 3
                    act.wait_ge(wtT_done, k + 1)
                    wait_last(act, o_mm, k)
                    a(wtT[:, :], ps_wT[:, 0, :], ACT.Copy)
                    a(gwT[:, :], ps_wT[0:EF, 1, :], ACT.Copy).then_inc(wtT_copied, 1)
                if has(i + 1):
                    k = i + 1
                    act.wait_ge(hT_done, k + 1)
                    wait_last(act, a_done, k)
                    a(hT_hi[:, :, :], ps_hT[:, :, :], ACT.Copy).then_inc(hT_hi_done, 1)
                if has(i + 2):
                    k = i + 2
                    act.wait_ge(rstd1, k + 1)
                    wait_last(act, hT_done, k)
                    a(h[:, :], xs[:, col(k), :].rearrange("p o d -> p (o d)"), ACT.Identity,
                      bias=mrs[:, 0, col(k)], scale=rs[:, 0, col(k)]).then_inc(normed1, 1)
                if has(i - 1):
                    k = i - 1
                    act.wait_ge(rstd2, k + 1)
                    wait_last(act, h2T_done, k)
                    a(h2[:, :, :], xs[:, col(k), :].rearrange("p o (q c) -> p c (o q)", c=KC),
                      ACT.Identity, bias=mrs[:, 1, col(k)], scale=rs[:, 1, col(k)]).then_inc(normed2, 1)
                if has(i - 2):
                    k = i - 2
                    act.wait_ge(gap_done, k + 1)
                    a(half_tanh[:, :], gap[:, :], ACT.Tanh, scale=0.5).then_inc(tanh_done, 1)

            pipeline(act, step)

        @block.vector
        def _(dve):
            v = nc.vector
            steps = [0]

            def step_(ins):
                steps[0] += 1
                ins.then_inc(s_route, 1)
                dve.wait_ge(s_route, steps[0])

            v.memset(ge[:, 0, :], 1.0)
            v.memset(ge[:, E, :], 0.0)
            v.memset(prev_end[:, 0:1], 0.0)
            v.memset(zeros[:, :], 0.0)
            dve.wait_ge(s_tok, 16)
            for e in range(1, E):
                last = v.tensor_scalar(ge[:, e, :], tok_i[:, :], float(e * PER_EXPERT), None, ALU.is_ge)
            step_(last)
            step_(v.tensor_tensor(member[:, :, :], ge[:, 0:E, :], ge[:, 1:E + 1, :], ALU.subtract))
            v.reduce_sum(per_row[:, :], member[:, :, :], axis=AX.X).then_inc(s_counts, 1)
            step_(v.tensor_tensor_scan(run[:, :], member[:, :, :].rearrange("p e c -> p (e c)"),
                                       zeros[:, :], 0.0, ALU.add, ALU.add))
            step_(v.tensor_copy(prev_end[:, 1:E],
                                run[:, :].rearrange("p (e c) -> p e c", c=C)[:, 0:E - 1, C - 1]))
            dve.wait_ge(s_const, 1)
            dve.wait_ge(s_rows_mm, 1)
            step_(v.tensor_tensor(over[:, :, :], ps_y[:, 0:E].unsqueeze(2).to_broadcast([P, E, C]),
                                  count_edge[:, :].unsqueeze(1).to_broadcast([P, E, C]), ALU.is_gt))
            step_(v.reduce_sum(tiles_of[:, :], over[:, :, :], axis=AX.X))
            step_(v.tensor_tensor_scan(tile_end[:, :], tiles_of[:, :], zeros[:, 0:E], 0.0,
                                       ALU.add, ALU.add))
            step_(v.tensor_tensor(first_slot[:, :], tile_end[:, :], tiles_of[:, :], ALU.subtract))
            step_(v.tensor_scalar(first_slot[:, :], first_slot[:, :], float(P), -1.0, ALU.mult, ALU.add))
            step_(v.tensor_tensor(shift[:, :], first_slot[:, :], prev_end[:, :], ALU.subtract))
            step_(v.tensor_tensor(shift[:, :], ps_a[:, 0:E], shift[:, :], ALU.add))
            step_(v.tensor_tensor(cand[:, :, :], run[:, :].rearrange("p (e c) -> p e c", c=C),
                                  shift[:, :].unsqueeze(2).to_broadcast([P, E, C]), ALU.add))
            step_(v.tensor_tensor(cand[:, :, :], cand[:, :, :], member[:, :, :], ALU.mult))
            step_(v.reduce_sum(slot1[:, :], cand[:, :, :].rearrange("p e c -> p c e"), axis=AX.X))
            step_(v.tensor_copy(slot_i[:, :], slot1[:, :]))
            v.tensor_scalar(tile_i[:, :], slot_i[:, :], 7, None, ALU.logical_shift_right)
            step_(v.tensor_scalar(in_tile_i[:, :], slot_i[:, :], P - 1, None, ALU.bitwise_and))
            v.tensor_copy(tile_f[:, :], tile_i[:, :])
            step_(v.tensor_copy(in_tile_f[:, :], in_tile_i[:, :]))
            step_(v.tensor_tensor(is_tile[:, :, :], tile_f[:, :].unsqueeze(2).to_broadcast([P, C, T]),
                                  tile_no[:, :].unsqueeze(1).to_broadcast([P, C, T]), ALU.is_equal))
            v.tensor_tensor(hot_tile[:, :, :], is_tile[:, :, :],
                            row_id1[:, :].unsqueeze(2).to_broadcast([P, C, T]), ALU.mult)
            v.tensor_tensor(hot_slot[:, :, :], in_tile_f[:, :].unsqueeze(2).to_broadcast([P, C, P]),
                            slot_no[:, :].unsqueeze(1).to_broadcast([P, C, P]),
                            ALU.is_equal).then_inc(s_hot, 1)
            for e in range(E - 1):
                last = v.tensor_scalar(past[:, e, :], tile_no[:, :], tile_end[:, e:e + 1], None, ALU.is_ge)
            step_(last)
            step_(v.reduce_sum(expert_f[:, :], past[:, :, :].rearrange("p e t -> p t e"), axis=AX.X))
            v.tensor_copy(expert_i[:, :], expert_f[:, :]).then_inc(s_expert, 1)
            dve.wait_ge(s_rows_mm, 2)
            step_(v.tensor_copy(row1[:, :], ps_pT[:, 0, 0:T]))
            v.tensor_scalar(gather_rows[:, :], row1[:, :], -1.0, 0.0, ALU.add, ALU.max)\
             .then_inc(s_gather_rows, 1)
            step_(v.tensor_scalar(pad[:, :], row1[:, :], 0.0, float(SKIP), ALU.is_equal, ALU.mult))
            step_(v.tensor_tensor(scatter_f[:, :], row1[:, :], pad[:, :], ALU.add))
            v.tensor_scalar(scatter_rows[:, :], scatter_f[:, :], -1.0, None, ALU.add)\
             .then_inc(s_scatter_rows, 1)
            dve.wait_ge(s_sq, E * KC)
            v.reduce_max(part_sq[:, :], row_sq[:, :], axis=AX.X).then_inc(s_partsq, 1)
            dve.wait_ge(s_sqT, 1)
            v.reduce_max(top_sq[:, :], ps_h2T[0:1, 0, :], axis=AX.X).then_inc(s_topsq, 1)
            dve.wait_ge(s_topall, 1)
            step_(v.tensor_copy(top_all[:, :], ps_o[:, 0:1]))
            step_(v.tensor_scalar(half_exp[:, :], top_all[:, :].bitcast(i32), 24, None,
                                  ALU.logical_shift_right))
            v.tensor_scalar(scale_w[:, :], half_exp[:, :], -ONE_EXP, SB * ONE_EXP, ALU.mult, ALU.add)
            step_(v.tensor_scalar(scale_inv[:, :], half_exp[:, :], ONE_EXP, (254 - SB) * ONE_EXP,
                                  ALU.mult, ALU.add))
            v.tensor_scalar(p_coef[:, :], s_w, 2.0 ** -PK, None, ALU.mult).then_inc(s_scale, 1)
            step_(v.tensor_tensor(inv2[:, :], s_inv, s_inv, ALU.mult))
            step_(v.tensor_tensor(inv3[:, :], inv2[:, :], s_inv, ALU.mult))
            dve.wait_ge(s_gates, 1)
            step_(v.tensor_scalar(y_coef[:, :], inv3[:, :], gates[:, 0:1], 2.0 ** PK, ALU.mult, ALU.mult))
            v.tensor_copy(w_in[:, :, 0:ER].rearrange("p c (e r) -> p e c r", r=R), wd_nat[:, :, :, :])
            v.tensor_copy(w_in[:, :, ER:HC], wr_nat[:, :, :])
            step_(v.tensor_scalar(b_in[:, ER:HC], b_in[:, ER:HC], BONUS, None, ALU.add))
            v.memset(w_top[:, :], 0.0).then_inc(s_ffn_w, 1)
            banks = [ps_hT, ps_wT]
            for n in range(E * KC):
                dve.wait_ge(s_whi, n + 1)
                v.scalar_tensor_tensor(w_lo[:, n // KC, n % KC, :],
                                       banks[n % 2][:, :, :].rearrange("p c q -> p (c q)"), s_w,
                                       w_hi[:, n // KC, n % KC, :], ALU.mult, ALU.subtract)\
                 .then_inc(s_wlo, 1)

            def gate(n):
                v.memset(gate_cell[:, n:n + 1], 0.0)

            def step(i, has):
                def stats_of_x():
                    k = i + 3
                    dve.wait_ge(x_in, k + 1)
                    wait_last(dve, aggr1, k)
                    gate(0)
                    v.bn_stats(st1[:, :], xs[:, col(k), :].rearrange("p o d -> p (o d)")).then_inc(stats1, 1)
                    dve.wait_ge(stats1, k + 1)
                    wait_last(dve, rstd1, k)
                    gate(1)
                    v.bn_aggr(mv1[:, :], st1[:, :]).then_inc(aggr1, 1)

                if has(i - 1):
                    k = i - 1
                    dve.wait_ge(pT_hi_done, k + 1)
                    v.tensor_tensor(pT_lo[:, :, :], ps_pT[:, :, :], pT_hi[:, :, :],
                                    ALU.subtract).then_inc(pT_lo_done, 1)
                if has(i):
                    k = i
                    dve.wait_ge(silu_done, k + 1)
                    v.scalar_tensor_tensor(prod[:, :], ps_a[:, :], p_coef[:, :], silu[:, :],
                                           ALU.mult, ALU.mult).then_inc(prod_done, 1)
                if has(i + 1):
                    k = i + 1
                    dve.wait_ge(hT_hi_done, k + 1)
                    v.tensor_tensor(hT_lo[:, :, :], ps_hT[:, :, :], hT_hi[:, :, :],
                                    ALU.subtract).then_inc(hT_lo_done, 1)
                if has(i - 1):
                    k = i - 1
                    row = xs[:, col(k), :].rearrange("p o d -> p (o d)")
                    dve.wait_ge(y_done, k + 1)
                    v.scalar_tensor_tensor(row, ps_y[:, :], y_coef[:, :], row,
                                           ALU.mult, ALU.add).then_inc(x1_done, 1)
                    dve.wait_ge(x1_done, k + 1)
                    wait_last(dve, aggr2, k)
                    gate(2)
                    v.bn_stats(st2[:, :], row).then_inc(stats2, 1)
                    dve.wait_ge(stats2, k + 1)
                    wait_last(dve, rstd2, k)
                    gate(3)
                    v.bn_aggr(mv2[:, :], st2[:, :]).then_inc(aggr2, 1)
                if has(i - 2):
                    k = i - 2
                    dve.wait_ge(hid_mm, k + 1)
                    wait_last(dve, weighted_done, k)
                    v.tensor_tensor(hid[:, :], ps_hid[:, 0:HC], b_in[:, :], ALU.add).then_inc(hid_done, 1)
                    dve.wait_ge(hid_done, k + 1)
                    if has(i + 3):
                        stats_of_x()
                    gate(4)
                    v.max(top8[:, :], hid[:, ER:HC]).then_inc(top_done, 1)
                    dve.wait_ge(top_done, k + 1)
                    v.tensor_tensor(gap[:, :], top8[:, 0:1], top8[:, 1:2], ALU.subtract).then_inc(gap_done, 1)
                    v.max_index(arg8[:, :], top8[:, :], hid[:, ER:HC]).then_inc(arg_done, 1)
                    dve.wait_ge(arg_done, k + 1)
                    v.tensor_copy(arg8f[:, :], arg8[:, :]).then_inc(argf_done, 1)
                    dve.wait_ge(tanh_done, k + 1)
                    v.tensor_scalar(w_top[:, 0:1], half_tanh[:, :], 0.5, 0.5, ALU.mult, ALU.add)
                    v.tensor_scalar(w_top[:, 1:2], half_tanh[:, :], -0.5, 0.5, ALU.mult, ALU.add)\
                     .then_inc(wtop_done, 1)
                    dve.wait_ge(wtop_done, k + 1)
                    v.tensor_scalar(w_first[:, :], slot_no[:, 0:EF], arg8f[:, 0:1], w_top[:, 0:1],
                                    ALU.is_equal, ALU.mult)
                    v.tensor_scalar(w_second[:, :], slot_no[:, 0:EF], arg8f[:, 1:2], w_top[:, 1:2],
                                    ALU.is_equal, ALU.mult).then_inc(wsecond_done, 1)
                    dve.wait_ge(wsecond_done, k + 1)
                    wait_last(dve, wtT_done, k)
                    v.tensor_tensor(weighted[:, ER:HC], w_first[:, :], w_second[:, :],
                                    ALU.add).then_inc(gate_w_done, 1)
                    dve.wait_ge(gate_w_done, k + 1)
                    v.scalar_tensor_tensor(
                        weighted[:, 0:ER].rearrange("p (e r) -> p e r", r=R),
                        hid[:, 0:ER].rearrange("p (e r) -> p e r", r=R), 0.0,
                        weighted[:, ER:HC].unsqueeze(2).to_broadcast([P, EF, R]),
                        ALU.max, ALU.mult).then_inc(weighted_done, 1)
                elif has(i + 3):
                    stats_of_x()
                if has(i - 3):
                    k = i - 3
                    row = xs[:, col(k), :].rearrange("p o d -> p (o d)")
                    dve.wait_ge(o_mm, k + 1)
                    v.scalar_tensor_tensor(row, ps_o[:, :], gates[:, 1:2], row,
                                           ALU.mult, ALU.add).then_inc(out_done, 1)

            pipeline(dve, step)


_INS = ['x', 'itok_BxS_13_99985', 'ctx_2048', 'g_xattn', 'g_ffn', 'L0_ffn_Wr', 'L0_ffn_br',
        'L0_ffn_Wd', 'L0_ffn_bd', 'L0_ffn_Wu', 'L0_ffn_bu']
_OUTS = [((4, 512, 512), 'float32')]


def kernel(**inputs):
    import numpy as _np
    import concourse.bacc as _bacc
    from concourse import mybir as _mybir
    from concourse.bass_utils import run_bass_kernel_spmd as _run

    nc = _bacc.Bacc("TRN2", target_bir_lowering=False, num_devices=1)
    arrays, args = {}, []
    for name in _INS:
        a = _np.ascontiguousarray(inputs[name])
        arrays[f"in_{name}_dram"] = a
        args.append(nc.dram_tensor(f"in_{name}_dram", a.shape, _mybir.dt.from_np(a.dtype), kind="ExternalInput").ap())
    for i, (shape, dtype) in enumerate(_OUTS):
        dt = _mybir.dt.from_np(_np.dtype(dtype))
        args.append(nc.dram_tensor(f"out_{i}_dram", shape, dt, kind="ExternalOutput").ap())
    bass_flamingo_gated_kernel(nc, *args)
    r = _run(nc, [arrays], core_ids=[0])
    got = tuple(r.results[0][f"out_{i}_dram"] for i in range(len(_OUTS)))
    return got[0]
```

```python
import numpy as np
import concourse.bass as bass
from concourse import mybir
from contextlib import ExitStack


def bass_flamingo_gated_kernel(
    nc: bass.Bass,
    x: bass.AP,
    tok: bass.AP,
    ctx_w: bass.AP,
    g_xattn: bass.AP,
    g_ffn: bass.AP,
    Wr: bass.AP,
    br: bass.AP,
    Wd: bass.AP,
    bd: bass.AP,
    Wu: bass.AP,
    bu: bass.AP,
    out: bass.AP,
):
    fp32, fp16 = mybir.dt.float32, mybir.dt.float16
    i32, u32 = mybir.dt.int32, mybir.dt.uint32
    ALU = mybir.AluOpType
    ACT = mybir.ActivationFunctionType
    AX = mybir.AxisListType

    P = 128
    B, S, D = x.shape
    N = B * S
    E = ctx_w.shape[0]
    KC = D // P
    C = N // P
    T = N // P + E - 1
    VOCAB = 25000
    PER_EXPERT = VOCAB // E
    EF, _, R = Wd.shape
    ER = EF * R
    HC = ER + EF
    BONUS = 3.0 * (1.0 - min(1 / 1250, 1.0))
    EPS = 1e-5
    SKIP = 2 * N

    WK = 10
    PK = 15
    SB = 127 + 63 + WK
    ONE_EXP = float(1 << 23)

    x_rows = x.rearrange("b s d -> (b s) d")
    out_rows = out.rearrange("b s d -> (b s) d")

    ctx = ExitStack()
    with ctx:
        def sb(name, shape, dt=fp32):
            return ctx.enter_context(nc.sbuf_tensor(name, shape, dt))

        def pb(name, shape, dt=fp32):
            return ctx.enter_context(nc.psum_tensor(name, shape, dt))

        def sem(name):
            return ctx.enter_context(nc.semaphore(name))

        ident = sb("ident", [P, P])
        before = sb("before", [P, P])
        ones = sb("ones", [P, P])
        slot_no = sb("slot_no", [P, P])
        tile_no = sb("tile_no", [P, T])
        count_edge = sb("count_edge", [P, C])
        row_id1 = sb("row_id1", [P, C])

        tok_i = sb("tok_i", [P, C], i32)
        ge = sb("ge", [P, E + 1, C])
        member = sb("member", [P, E, C])
        zeros = sb("zeros", [P, E * C])
        run = sb("run", [P, E * C])
        per_row = sb("per_row", [P, E])
        prev_end = sb("prev_end", [P, E])
        over = sb("over", [P, E, C])
        tiles_of = sb("tiles_of", [P, E])
        tile_end = sb("tile_end", [P, E])
        first_slot = sb("first_slot", [P, E])
        shift = sb("shift", [P, E])
        cand = sb("cand", [P, E, C])
        slot1 = sb("slot1", [P, C])
        slot_i = sb("slot_i", [P, C], i32)
        tile_i = sb("tile_i", [P, C], i32)
        in_tile_i = sb("in_tile_i", [P, C], i32)
        tile_f = sb("tile_f", [P, C])
        in_tile_f = sb("in_tile_f", [P, C])
        hot_slot = sb("hot_slot", [P, C, P], fp16)
        hot_tile = sb("hot_tile", [P, C, T], fp16)
        is_tile = sb("is_tile", [P, C, T])
        row1 = sb("row1", [P, T])
        pad = sb("pad", [P, T])
        gather_rows = sb("gather_rows", [P, T], u32)
        scatter_f = sb("scatter_f", [P, T])
        scatter_rows = sb("scatter_rows", [P, T], u32)
        past = sb("past", [P, E - 1, T])
        expert_f = sb("expert_f", [P, T])
        expert_i = sb("expert_i", [P, T], i32)

        w_nat = sb("w_nat", [P, E, KC, D])
        w_hi = sb("w_hi", [P, E, KC, D], fp16)
        w_lo = sb("w_lo", [P, E, KC, D], fp16)
        sq_act = sb("sq_act", [P, D])
        sq_dve = sb("sq_dve", [P, D])
        row_sq = sb("row_sq", [P, E, KC])
        part_sq = sb("part_sq", [P, E])
        top_sq = sb("top_sq", [1, E])
        top_all = sb("top_all", [P, E])
        half_exp = sb("half_exp", [P, E], i32)
        half_exp_f = sb("half_exp_f", [P, E])
        scale_w = sb("scale_w", [P, E], i32)
        s_w = scale_w[:, :].bitcast(fp32)
        exp_of = sb("exp_of", [P, E, T])
        exp_t = sb("exp_t", [P, T])
        inv_bits = sb("inv_bits", [P, T], i32)
        prod_bits = sb("prod_bits", [P, T], i32)
        inv_t = inv_bits[:, :].bitcast(fp32)
        prod_t = prod_bits[:, :].bitcast(fp32)
        inv2 = sb("inv2", [P, T])
        inv3 = sb("inv3", [P, T])
        y_t = sb("y_t", [P, T])
        gates_in = sb("gates_in", [P, 2])
        gates = sb("gates", [P, 2])

        wd_nat = sb("wd_nat", [P, EF, KC, R])
        wr_nat = sb("wr_nat", [P, KC, EF])
        w_in_hi = sb("w_in_hi", [P, KC, HC], fp16)
        w_in_lo = sb("w_in_lo", [P, KC, HC], fp16)
        b_in = sb("b_in", [P, HC])
        b_s = sb("b_s", [P, HC])
        wu_nat = sb("wu_nat", [ER, D])
        wu_hi = sb("wu_hi", [ER, D], fp16)
        wu_lo = sb("wu_lo", [ER, D], fp16)
        Q = 32
        Q3 = 3 * Q
        bu_nat = sb("bu_nat", [Q3, D])
        bu3 = sb("bu3", [Q3, D], fp16)
        sq_parts = sb("sq_parts", [P, 5])
        ffn_parts = sb("ffn_parts", [P, 2])
        ffn_tot = sb("ffn_tot", [P, 2])
        ffn_half = sb("ffn_half", [P, 2], i32)
        ffn_bits = sb("ffn_bits", [P, 2], i32)
        ffn_inv_bits = sb("ffn_inv_bits", [P, 2], i32)
        s_ffn = ffn_bits[:, :].bitcast(fp32)
        s_ffn_inv = ffn_inv_bits[:, :].bitcast(fp32)
        half_inv = sb("half_inv", [P, 1])
        inv_both = sb("inv_both", [P, 1])
        out_coef = sb("out_coef", [P, 1])

        xs = sb("xs", [P, T, D])
        st1 = sb("st1", [P, 6])
        mv1 = sb("mv1", [P, 2])
        st2 = sb("st2", [P, 6])
        mv2 = sb("mv2", [P, 2])
        ve = sb("ve", [P, 2, T])
        rs = sb("rs", [P, 2, T])
        mrs = sb("mrs", [P, 2, T])
        neg_half = sb("neg_half", [P, 1])
        h = sb("h", [P, D])
        hT_hi = sb("hT_hi", [P, KC, P], fp16)
        hT_lo = sb("hT_lo", [P, KC, P], fp16)
        silu = sb("silu", [P, D])
        prod = sb("prod", [P, D])
        pT_hi = sb("pT_hi", [P, KC, P], fp16)
        pT_lo = sb("pT_lo", [P, KC, P], fp16)
        h2 = sb("h2", [P, KC, P])
        h2T_hi = sb("h2T_hi", [P, KC, P], fp16)
        h2T_lo = sb("h2T_lo", [P, KC, P], fp16)
        hid = sb("hid", [P, HC])
        top8 = sb("top8", [P, 8])
        arg8 = sb("arg8", [P, 8], u32)
        arg8f = sb("arg8f", [P, 8])
        gate_cell = sb("gate_cell", [P, 5])
        gap = sb("gap", [P, 1])
        half_tanh = sb("half_tanh", [P, 1])
        half_first = sb("half_first", [P, EF])
        half_second = sb("half_second", [P, EF])
        half_sum = sb("half_sum", [P, EF])
        half_dif = sb("half_dif", [P, EF])
        w8 = sb("w8", [P, EF])
        weighted = sb("weighted", [P, ER])
        w_rep = sb("w_rep", [P, 3, Q])
        wtT_hi = sb("wtT_hi", [P, P], fp16)
        wtT_lo = sb("wtT_lo", [P, P], fp16)
        gwT = sb("gwT", [Q3, P], fp16)

        ps_hT = pb("ps_hT", [P, KC, P])
        ps_a = pb("ps_a", [P, D])
        ps_pT = pb("ps_pT", [P, KC, P])
        ps_y = pb("ps_y", [P, D])
        ps_h2T = pb("ps_h2T", [P, KC, P])
        ps_hid = pb("ps_hid", [P, D])
        ps_wT = pb("ps_wT", [P, KC, P])
        ps_o = pb("ps_o", [P, D])

        s_tok = sem("s_tok")
        s_wload = [sem(f"s_wload{e}") for e in range(E)]
        s_small = sem("s_small")
        s_gather = [sem(f"s_gather{t}") for t in range(T)]
        s_scatter = sem("s_scatter")
        s_const = sem("s_const")
        s_pool = sem("s_pool")
        s_route = sem("s_route")
        s_counts = sem("s_counts")
        s_rows_mm = sem("s_rows_mm")
        s_hot = sem("s_hot")
        s_gather_rows = sem("s_gather_rows")
        s_scatter_rows = sem("s_scatter_rows")
        s_expert = sem("s_expert")
        s_sq = sem("s_sq")
        s_partsq = sem("s_partsq")
        s_sqT = sem("s_sqT")
        s_topsq = sem("s_topsq")
        s_topall = sem("s_topall")
        s_scale = sem("s_scale")
        s_gates = sem("s_gates")
        s_tables = sem("s_tables")
        s_wT = sem("s_wT")
        s_whi = sem("s_whi")
        s_wlo = sem("s_wlo")
        s_sqd = sem("s_sqd")
        s_ffn_sq = sem("s_ffn_sq")
        s_ffn_part = sem("s_ffn_part")
        s_ffn_tot = sem("s_ffn_tot")
        s_ffn_scale = sem("s_ffn_scale")
        s_ffn_hi = sem("s_ffn_hi")
        s_ffn_w = sem("s_ffn_w")
        x_in = sem("x_in")
        stats1 = sem("stats1")
        aggr1 = sem("aggr1")
        rstd1 = sem("rstd1")
        normed1 = sem("normed1")
        hT_done = sem("hT_done")
        hT_hi_done = sem("hT_hi_done")
        hT_lo_done = sem("hT_lo_done")
        a_done = sem("a_done")
        silu_done = sem("silu_done")
        prod_done = sem("prod_done")
        pT_done = sem("pT_done")
        pT_hi_done = sem("pT_hi_done")
        pT_lo_done = sem("pT_lo_done")
        y_done = sem("y_done")
        x1_done = sem("x1_done")
        stats2 = sem("stats2")
        aggr2 = sem("aggr2")
        rstd2 = sem("rstd2")
        rs_step = sem("rs_step")
        normed2 = sem("normed2")
        h2T_done = sem("h2T_done")
        h2T_hi_done = sem("h2T_hi_done")
        h2T_lo_done = sem("h2T_lo_done")
        hid_mm = sem("hid_mm")
        hid_done = sem("hid_done")
        top_done = sem("top_done")
        arg_done = sem("arg_done")
        argf_done = sem("argf_done")
        gap_done = sem("gap_done")
        tanh_done = sem("tanh_done")
        halves_done = sem("halves_done")
        mix_done = sem("mix_done")
        w8_done = sem("w8_done")
        weighted_done = sem("weighted_done")
        wtT_done = sem("wtT_done")
        wtT_hi_done = sem("wtT_hi_done")
        wtT_lo_done = sem("wtT_lo_done")
        o_mm = sem("o_mm")
        out_done = sem("out_done")

        block = ctx.enter_context(nc.Block())

        FULL0, FULL1 = 3, T - 3
        FIRST, LAST = -3, T + 3

        def some(k):
            return 0 <= k < T

        def pipeline(eng, step, first, lag=3):
            for i in range(first, lag):
                step(i, some)
            with eng.Fori(lag, FULL1) as i:
                step(i, lambda k: True)
            for i in range(FULL1, T + lag):
                step(i, some)

        def col(k):
            return bass.ds(k, 1)

        def wait_last(eng, done, k):
            if not (isinstance(k, int) and k == 0):
                eng.wait_ge(done, k)

        AHEAD = 4
        w_banks = [ps_wT, ps_pT, ps_y, ps_o]
        ACT_SQ = [KC, KC] + [KC - 1] * (E - 2)
        GROUPS = [(0, 1), (1, 2), (2, 4)]
        group_of = [n for n, (e0, e1) in enumerate(GROUPS) for _ in range(e0, e1)]
        act_sq_until = [sum(ACT_SQ[:e + 1]) for e in range(E)]

        @block.sync
        def _(sp):
            sp.dma_start(tok_i[:, :], tok.rearrange("b (q c) -> (b q) c", c=C)).then_inc(s_tok, 16)
            for e in range(E):
                sp.dma_start(w_nat[:, e, :, :], ctx_w[e, :, :].rearrange("(c p) k -> p c k", p=P))\
                  .then_inc(s_wload[e], 16)
            sp.dma_start(gates_in[:, 0:1], g_xattn.rearrange("(a n) -> a n", a=1).to_broadcast([P, 1])).then_inc(s_small, 16)
            sp.dma_start(gates_in[:, 1:2], g_ffn.rearrange("(a n) -> a n", a=1).to_broadcast([P, 1])).then_inc(s_small, 16)
            sp.dma_start(b_in[:, 0:ER], bd.rearrange("(a e) r -> a (e r)", a=1).to_broadcast([P, ER])).then_inc(s_small, 16)
            sp.dma_start(b_in[:, ER:HC], br.rearrange("(a e) -> a e", a=1).to_broadcast([P, EF])).then_inc(s_small, 16)
            sp.dma_start(wr_nat[:, :, :], Wr.rearrange("(p c) e -> p c e", c=KC)).then_inc(s_small, 16)
            sp.dma_start(wd_nat[:, :, :, :], Wd.rearrange("e (p c) r -> p e (c r)", c=KC)).then_inc(s_small, 16)
            sp.dma_start(wu_nat[:, :], Wu.rearrange("e r d -> (e r) d")).then_inc(s_small, 16)
            sp.wait_ge(s_const, 2)
            for n in range(3):
                sp.dma_start(bu_nat[n * Q:n * Q + EF, :], bu[:, :]).then_inc(s_small, 16)
            for t in range(T):
                sp.wait_ge(s_gather[t], 16)
                sp.sem_inc(x_in, 1)
            sp.wait_ge(s_scatter, 16 * T)

        @block.gpsimd
        def _(pool):
            g = nc.gpsimd
            g.memset(neg_half[:, :], -0.5).then_inc(s_pool, 1)
            g.memset(before[:, :], 1.0).then_inc(s_pool, 1)
            g.memset(ident[:, :], 0.0).then_inc(s_pool, 1)
            g.memset(ones[:, :], 1.0)
            g.iota(count_edge[:, :], pattern=[[P, C]], base=0, channel_multiplier=0,
                   allow_small_or_imprecise_dtypes=True)
            pool.wait_ge(s_pool, 3)
            g.affine_select(out=ident[:, :], in_=ident[:, :], compare_op=ALU.not_equal, fill=1.0,
                            base=0, pattern=[[-1, P]], channel_multiplier=1)
            g.affine_select(out=before[:, :], in_=before[:, :], compare_op=ALU.is_gt, fill=0.0,
                            base=0, pattern=[[1, P]], channel_multiplier=-1)
            g.iota(row_id1[:, :], pattern=[[1, C]], base=1, channel_multiplier=C,
                   allow_small_or_imprecise_dtypes=True)
            g.iota(tile_no[:, :], pattern=[[1, T]], base=0, channel_multiplier=0,
                   allow_small_or_imprecise_dtypes=True)
            g.iota(slot_no[:, :], pattern=[[1, P]], base=0, channel_multiplier=0,
                   allow_small_or_imprecise_dtypes=True).then_inc(s_const, 1)
            g.memset(bu_nat[:, :], 0.0)
            g.memset(w_rep[:, :, :], 0.0)
            g.memset(sq_parts[:, :], 0.0).then_inc(s_const, 1)
            pool.wait_ge(s_gather_rows, 1)

            def gather(t):
                if t < T:
                    g.indirect_dma_start(
                        out=xs[:, t, :], out_offset=None, in_=x_rows[:, :],
                        in_offset=bass.IndirectOffsetOnAxis(ap=gather_rows[:, t:t + 1], axis=0),
                    ).then_inc(s_gather[t], 16)

            for t in range(AHEAD):
                gather(t)
            steps = [0]

            def then(ins):
                steps[0] += 1
                ins.then_inc(rs_step, 1)
                pool.wait_ge(rs_step, steps[0])

            def rstd(n, mv, k, done):
                then(g.tensor_scalar(ve[:, n, k:k + 1], mv[:, 1:2], EPS, None, ALU.add))
                then(g.tensor_tensor(rs[:, n, k:k + 1], ve[:, n, k:k + 1], neg_half[:, :], ALU.pow))
                g.tensor_scalar(mrs[:, n, k:k + 1], mv[:, 0:1], -1.0, rs[:, n, k:k + 1],
                                ALU.mult, ALU.mult).then_inc(done, 1)

            for i in range(FIRST, LAST):
                if 0 <= i + 3 < T:
                    pool.wait_ge(aggr1, i + 4)
                    rstd(0, mv1, i + 3, rstd1)
                gather(i + 3 + AHEAD)
                if 0 <= i - 1 < T:
                    pool.wait_ge(aggr2, i)
                    rstd(1, mv2, i - 1, rstd2)
                if i == 0:
                    pool.wait_ge(s_scatter_rows, 1)
                if 0 <= i - 3 < T:
                    pool.wait_ge(out_done, i - 2)
                    g.indirect_dma_start(
                        out=out_rows[:, :],
                        out_offset=bass.IndirectOffsetOnAxis(ap=scatter_rows[:, i - 3:i - 2], axis=0),
                        in_=xs[:, i - 3, :], in_offset=None,
                        bounds_check=N - 1, oob_is_err=False,
                    ).then_inc(s_scatter, 16)

        @block.tensor
        def _(pe):
            mm, tr = nc.tensor.matmul, nc.tensor.transpose

            def w_blocks(e):
                pe.wait_ge(s_wload[e], 16)
                for kc in range(KC):
                    if e:
                        pe.wait_ge(s_wlo, (e - 1) * KC + kc + 1)
                    for c in range(KC):
                        last = tr(w_banks[kc][:, c, :] if len(w_banks[kc].shape) == 3
                                  else w_banks[kc][:, c * P:(c + 1) * P],
                                  w_nat[:, e, c, kc * P:(kc + 1) * P], ident[:, :])
                    last.then_inc(s_wT, 1)

            def top_norms(n):
                e0, e1 = GROUPS[n]
                pe.wait_ge(s_partsq, n + 1)
                for e in range(e0, e1):
                    last = tr(ps_h2T[0:1, e - e0, :], part_sq[:, e:e + 1], ident[:, :])
                last.then_inc(s_sqT, 1)
                pe.wait_ge(s_topsq, n + 1)
                mm(ps_h2T[:, 2, e0:e1], ones[0:1, :], top_sq[:, e0:e1],
                   start=True, stop=True).then_inc(s_topall, 1)

            pe.wait_ge(s_const, 1)
            pe.wait_ge(s_counts, 1)
            mm(ps_hid[:, 0:E], before[:, :], per_row[:, :], start=True, stop=True)
            mm(ps_hid[:, E:2 * E], ones[:, :], per_row[:, :], start=True, stop=True).then_inc(s_rows_mm, 1)
            w_blocks(0)
            pe.wait_ge(s_hot, 1)
            for c in range(C):
                last = mm(ps_hT[:, 0, 0:T], hot_slot[:, c, :], hot_tile[:, c, :],
                          start=(c == 0), stop=(c == C - 1))
            last.then_inc(s_rows_mm, 1)
            top_norms(0)
            top_norms(1)
            w_blocks(1)
            top_norms(2)
            w_blocks(2)

            def split_product(ps, lhs_hi, lhs_lo, e):
                for kc in range(KC):
                    hi = w_hi[:, bass.ds(e, 1), kc, :].rearrange("p e n -> p (e n)")
                    lo = w_lo[:, bass.ds(e, 1), kc, :].rearrange("p e n -> p (e n)")
                    mm(ps[:, :], lhs_hi[:, kc, :], hi, start=(kc == 0), stop=False)
                    mm(ps[:, :], lhs_hi[:, kc, :], lo, start=False, stop=False)
                    last = mm(ps[:, :], lhs_lo[:, kc, :], hi, start=False, stop=(kc == KC - 1))
                return last

            def expert_of(k):
                return pe.value_load(expert_i[0:1, col(k)], min_val=0, max_val=E - 1)

            def step(i, has):
                e_last = expert_of(i - 1) if has(i - 1) else None
                e_now = expert_of(i) if has(i) else None
                if has(i - 3):
                    k = i - 3
                    pe.wait_ge(h2T_lo_done, k + 1)
                    wait_last(pe, hid_done, k)
                    for c in range(KC):
                        mm(ps_hid[:, 0:HC], h2T_hi[:, c, :], w_in_hi[:, c, :], start=(c == 0), stop=False)
                        mm(ps_hid[:, 0:HC], h2T_hi[:, c, :], w_in_lo[:, c, :], start=False, stop=False)
                        last = mm(ps_hid[:, 0:HC], h2T_lo[:, c, :], w_in_hi[:, c, :],
                                  start=False, stop=(c == KC - 1))
                    last.then_inc(hid_mm, 1)
                if has(i - 4):
                    k = i - 4
                    pe.wait_ge(wtT_lo_done, k + 1)
                    wait_last(pe, out_done, k)
                    mm(ps_o[:, :], wtT_hi[:, :], wu_hi[:, :], start=True, stop=False)
                    mm(ps_o[:, :], wtT_hi[:, :], wu_lo[:, :], start=False, stop=False)
                    mm(ps_o[:, :], wtT_lo[:, :], wu_hi[:, :], start=False, stop=False)
                    mm(ps_o[:, :], gwT[:, :], bu3[:, :], start=False, stop=True).then_inc(o_mm, 1)
                if has(i - 1):
                    k = i - 1
                    pe.wait_ge(prod_done, k + 1)
                    for c in range(KC):
                        last = tr(ps_pT[:, c, :], prod[:, c * P:(c + 1) * P], ident[:, :])
                    last.then_inc(pT_done, 1)
                if has(i):
                    k = i
                    if isinstance(k, int) and k == 0:
                        pe.wait_ge(s_wlo, (e_now + 1) * KC)
                    pe.wait_ge(hT_lo_done, k + 1)
                    split_product(ps_a, hT_hi, hT_lo, e_now).then_inc(a_done, 1)
                if has(i + 1):
                    k = i + 1
                    pe.wait_ge(normed1, k + 1)
                    for c in range(KC):
                        last = tr(ps_hT[:, c, :], h[:, c * P:(c + 1) * P], ident[:, :])
                    last.then_inc(hT_done, 1)
                if has(i - 2):
                    k = i - 2
                    pe.wait_ge(normed2, k + 1)
                    for c in range(KC):
                        last = tr(ps_h2T[:, c, :], h2[:, c, :], ident[:, :])
                    last.then_inc(h2T_done, 1)
                if has(i - 3):
                    k = i - 3
                    pe.wait_ge(weighted_done, k + 1)
                    wait_last(pe, wtT_lo_done, k)
                    tr(ps_wT[:, 0, :], weighted[:, :], ident[:, :])
                    tr(ps_wT[0:Q3, 1, :], w_rep[:, :, :].rearrange("p a q -> p (a q)"),
                       ident[:, :]).then_inc(wtT_done, 1)
                if has(i - 1):
                    k = i - 1
                    pe.wait_ge(pT_lo_done, k + 1)
                    wait_last(pe, x1_done, k)
                    split_product(ps_y, pT_hi, pT_lo, e_last).then_inc(y_done, 1)

            step(-1, some)
            w_blocks(3)
            pe.wait_ge(s_expert, 1)
            step(0, some)
            pe.wait_ge(s_wlo, E * KC)
            pe.wait_ge(s_ffn_part, 1)
            mm(ps_hid[:, 0:2], ones[:, :], ffn_parts[:, :], start=True, stop=True).then_inc(s_ffn_tot, 1)
            step(1, some)
            pe.wait_ge(s_ffn_w, 1)
            pipeline(pe, step, 2, lag=4)

        @block.scalar
        def _(act):
            a = nc.scalar.activation
            def square_sums(e):
                act.wait_ge(s_wload[e], 16)
                for c in range(ACT_SQ[e]):
                    n = 1 + (act_sq_until[e - 1] if e else 0) + c
                    act.wait_ge(s_sq, n)
                    a(sq_act[:, :], w_nat[:, e, c, :], ACT.Square,
                      accum_out=row_sq[:, e, c:c + 1]).then_inc(s_sq, 1)

            def high_parts(e):
                act.wait_ge(s_scale, group_of[e] + 1)
                for kc in range(KC):
                    act.wait_ge(s_wT, e * KC + kc + 1)
                    bank = w_banks[kc]
                    ps = bank[:, :, :].rearrange("p c q -> p (c q)") if len(bank.shape) == 3 else bank[:, :]
                    a(w_hi[:, e, kc, :], ps, ACT.Copy, scale=s_w[:, e:e + 1]).then_inc(s_whi, 1)

            def ffn_squares():
                act.wait_ge(s_small, 16 * 10)
                act.wait_ge(s_sq, 1 + act_sq_until[-1])
                parts = [(wd_nat[:, :, :, :], sq_act[:, :].rearrange("p (e c r) -> p e c r", c=KC, r=R), P),
                         (wr_nat[:, :, :], sq_act[:, 0:KC * EF].rearrange("p (c e) -> p c e", e=EF), P),
                         (b_in[0:1, :], sq_act[0:1, 0:HC], 1),
                         (wu_nat[:, :], sq_act[:, :], ER),
                         (bu_nat[0:EF, :], sq_act[0:EF, :], EF)]
                act.wait_ge(s_ffn_scale, 1)
                for n, (src, dst, rows) in enumerate(parts):
                    if n:
                        act.wait_ge(s_ffn_sq, n)
                    a(dst, src, ACT.Square, accum_out=sq_parts[0:rows, n:n + 1]).then_inc(s_ffn_sq, 1)

            def ffn_high_parts():
                act.wait_ge(s_ffn_scale, 2)
                a(w_in_hi[:, :, 0:ER].rearrange("p c (e r) -> p e c r", r=R), wd_nat[:, :, :, :],
                  ACT.Copy, scale=s_ffn[:, 0:1])
                a(w_in_hi[:, :, ER:HC], wr_nat[:, :, :], ACT.Copy, scale=s_ffn[:, 0:1])
                a(wu_hi[:, :], wu_nat[:, :], ACT.Copy, scale=s_ffn[:, 1:2])
                a(bu3[:, :], bu_nat[:, :], ACT.Copy, scale=s_ffn[0:Q3, 1:2]).then_inc(s_ffn_hi, 1)

            def step(i, has):
                if has(i - 1):
                    k = i - 1
                    act.wait_ge(pT_done, k + 1)
                    wait_last(act, y_done, k)
                    a(pT_hi[:, :, :], ps_pT[:, :, :], ACT.Copy).then_inc(pT_hi_done, 1)
                if has(i - 3):
                    k = i - 3
                    act.wait_ge(gap_done, k + 1)
                    a(half_tanh[:, :], gap[:, :], ACT.Tanh, scale=half_inv[:, :]).then_inc(tanh_done, 1)
                if has(i - 2):
                    k = i - 2
                    act.wait_ge(rstd2, k + 1)
                    wait_last(act, h2T_done, k)
                    a(h2[:, :, :], xs[:, col(k), :].rearrange("p o (q c) -> p c (o q)", c=KC),
                      ACT.Identity, bias=mrs[:, 1, col(k)], scale=rs[:, 1, col(k)]).then_inc(normed2, 1)
                if has(i):
                    k = i
                    act.wait_ge(a_done, k + 1)
                    a(silu[:, :], ps_a[:, :], ACT.Silu, scale=inv_t[:, col(k)]).then_inc(silu_done, 1)
                if has(i + 1):
                    k = i + 1
                    act.wait_ge(hT_done, k + 1)
                    wait_last(act, a_done, k)
                    a(hT_hi[:, :, :], ps_hT[:, :, :], ACT.Copy).then_inc(hT_hi_done, 1)
                if has(i - 2):
                    k = i - 2
                    act.wait_ge(h2T_done, k + 1)
                    wait_last(act, hid_mm, k)
                    a(h2T_hi[:, :, :], ps_h2T[:, :, :], ACT.Copy).then_inc(h2T_hi_done, 1)
                if has(i - 3):
                    k = i - 3
                    act.wait_ge(wtT_done, k + 1)
                    wait_last(act, o_mm, k)
                    a(wtT_hi[:, :], ps_wT[:, 0, :], ACT.Copy)
                    a(gwT[:, :], ps_wT[0:Q3, 1, :], ACT.Copy).then_inc(wtT_hi_done, 1)
                if has(i + 2):
                    k = i + 2
                    act.wait_ge(rstd1, k + 1)
                    wait_last(act, hT_done, k)
                    a(h[:, :], xs[:, col(k), :].rearrange("p o d -> p (o d)"), ACT.Identity,
                      bias=mrs[:, 0, col(k)], scale=rs[:, 0, col(k)]).then_inc(normed1, 1)

            act.wait_ge(s_pool, 1)
            a(sq_act[0:1, 0:1], neg_half[0:1, :], ACT.Silu).then_inc(s_sq, 1)
            act.wait_ge(s_sq, 1)
            square_sums(0)
            square_sums(1)
            square_sums(2)
            high_parts(0)
            square_sums(3)
            high_parts(1)
            act.wait_ge(s_small, 16 * 10)
            a(gates[:, :], gates_in[:, :], ACT.Tanh).then_inc(s_gates, 1)
            step(-2, some)
            high_parts(2)
            step(-1, some)
            high_parts(3)
            act.wait_ge(s_tables, 1)
            ffn_squares()
            step(0, some)
            ffn_high_parts()
            pipeline(act, step, 1)

        @block.vector
        def _(dve):
            v = nc.vector
            steps = [0]

            def then(ins):
                steps[0] += 1
                ins.then_inc(s_route, 1)
                dve.wait_ge(s_route, steps[0])

            v.memset(ge[:, 0, :], 1.0)
            v.memset(ge[:, E, :], 0.0)
            v.memset(prev_end[:, 0:1], 0.0)
            v.memset(zeros[:, :], 0.0)
            dve.wait_ge(s_tok, 16)
            for e in range(1, E):
                last = v.tensor_scalar(ge[:, e, :], tok_i[:, :], float(e * PER_EXPERT), None, ALU.is_ge)
            then(last)
            then(v.tensor_tensor(member[:, :, :], ge[:, 0:E, :], ge[:, 1:E + 1, :], ALU.subtract))
            v.reduce_sum(per_row[:, :], member[:, :, :], axis=AX.X).then_inc(s_counts, 1)
            then(v.tensor_tensor_scan(run[:, :], member[:, :, :].rearrange("p e c -> p (e c)"),
                                      zeros[:, :], 0.0, ALU.add, ALU.add))
            then(v.tensor_copy(prev_end[:, 1:E],
                               run[:, :].rearrange("p (e c) -> p e c", c=C)[:, 0:E - 1, C - 1]))
            dve.wait_ge(s_const, 1)
            dve.wait_ge(s_rows_mm, 1)
            then(v.tensor_tensor(over[:, :, :], ps_hid[:, E:2 * E].unsqueeze(2).to_broadcast([P, E, C]),
                                 count_edge[:, :].unsqueeze(1).to_broadcast([P, E, C]), ALU.is_gt))
            then(v.reduce_sum(tiles_of[:, :], over[:, :, :], axis=AX.X))
            then(v.tensor_tensor_scan(tile_end[:, :], tiles_of[:, :], zeros[:, 0:E], 0.0,
                                      ALU.add, ALU.add))
            then(v.tensor_tensor(first_slot[:, :], tile_end[:, :], tiles_of[:, :], ALU.subtract))
            then(v.tensor_scalar(first_slot[:, :], first_slot[:, :], float(P), -1.0, ALU.mult, ALU.add))
            then(v.tensor_tensor(shift[:, :], first_slot[:, :], prev_end[:, :], ALU.subtract))
            then(v.tensor_tensor(shift[:, :], ps_hid[:, 0:E], shift[:, :], ALU.add))
            then(v.tensor_tensor(cand[:, :, :], run[:, :].rearrange("p (e c) -> p e c", c=C),
                                 shift[:, :].unsqueeze(2).to_broadcast([P, E, C]), ALU.add))
            then(v.tensor_tensor(cand[:, :, :], cand[:, :, :], member[:, :, :], ALU.mult))
            then(v.reduce_sum(slot1[:, :], cand[:, :, :].rearrange("p e c -> p c e"), axis=AX.X))
            then(v.tensor_copy(slot_i[:, :], slot1[:, :]))
            v.tensor_scalar(tile_i[:, :], slot_i[:, :], 7, None, ALU.logical_shift_right)
            then(v.tensor_scalar(in_tile_i[:, :], slot_i[:, :], P - 1, None, ALU.bitwise_and))
            v.tensor_copy(tile_f[:, :], tile_i[:, :])
            then(v.tensor_copy(in_tile_f[:, :], in_tile_i[:, :]))
            then(v.tensor_tensor(is_tile[:, :, :], tile_f[:, :].unsqueeze(2).to_broadcast([P, C, T]),
                                 tile_no[:, :].unsqueeze(1).to_broadcast([P, C, T]), ALU.is_equal))
            v.tensor_tensor(hot_tile[:, :, :], is_tile[:, :, :],
                            row_id1[:, :].unsqueeze(2).to_broadcast([P, C, T]), ALU.mult)
            v.tensor_tensor(hot_slot[:, :, :], in_tile_f[:, :].unsqueeze(2).to_broadcast([P, C, P]),
                            slot_no[:, :].unsqueeze(1).to_broadcast([P, C, P]),
                            ALU.is_equal).then_inc(s_hot, 1)

            def square_sums(e):
                dve.wait_ge(s_wload[e], 16)
                for c in range(ACT_SQ[e], KC):
                    then(v.tensor_tensor_reduce(
                        out=sq_dve[:, :], in0=w_nat[:, e, c, :], in1=w_nat[:, e, c, :], scale=1.0,
                        scalar=0.0, op0=ALU.mult, op1=ALU.add, accum_out=row_sq[:, e, c:c + 1]))

            def top_rows(n):
                e0, e1 = GROUPS[n]
                dve.wait_ge(s_sq, 1 + act_sq_until[e1 - 1])
                v.reduce_max(part_sq[:, e0:e1], row_sq[:, e0:e1, :], axis=AX.X).then_inc(s_partsq, 1)

            def scales(n):
                e0, e1 = GROUPS[n]
                dve.wait_ge(s_sqT, n + 1)
                v.reduce_max(top_sq[:, e0:e1], ps_h2T[0:1, 0:e1 - e0, :], axis=AX.X).then_inc(s_topsq, 1)
                dve.wait_ge(s_topall, n + 1)
                then(v.tensor_copy(top_all[:, e0:e1], ps_h2T[:, 2, e0:e1]))
                then(v.tensor_scalar(half_exp[:, e0:e1], top_all[:, e0:e1].bitcast(i32), 24, None,
                                     ALU.logical_shift_right))
                v.tensor_scalar(scale_w[:, e0:e1], half_exp[:, e0:e1], -ONE_EXP, SB * ONE_EXP,
                                ALU.mult, ALU.add).then_inc(s_scale, 1)

            def low_parts(e, blocks=range(KC)):
                for kc in blocks:
                    dve.wait_ge(s_whi, e * KC + kc + 1)
                    bank = w_banks[kc]
                    ps = bank[:, :, :].rearrange("p c q -> p (c q)") if len(bank.shape) == 3 else bank[:, :]
                    v.scalar_tensor_tensor(w_lo[:, e, kc, :], ps, s_w[:, e:e + 1], w_hi[:, e, kc, :],
                                           ALU.mult, ALU.subtract).then_inc(s_wlo, 1)

            def row_numbers():
                dve.wait_ge(s_rows_mm, 2)
                then(v.tensor_copy(row1[:, :], ps_hT[:, 0, 0:T]))
                v.tensor_scalar(gather_rows[:, :], row1[:, :], -1.0, 0.0, ALU.add, ALU.max)\
                 .then_inc(s_gather_rows, 1)
                then(v.tensor_scalar(pad[:, :], row1[:, :], 0.0, float(SKIP), ALU.is_equal, ALU.mult))
                then(v.tensor_tensor(scatter_f[:, :], row1[:, :], pad[:, :], ALU.add))
                v.tensor_scalar(scatter_rows[:, :], scatter_f[:, :], -1.0, None, ALU.add)\
                 .then_inc(s_scatter_rows, 1)

            def experts():
                for e in range(E - 1):
                    last = v.tensor_scalar(past[:, e, :], tile_no[:, :], tile_end[:, e:e + 1], None, ALU.is_ge)
                then(last)
                then(v.reduce_sum(expert_f[:, :], past[:, :, :].rearrange("p e t -> p t e"), axis=AX.X))
                v.tensor_copy(expert_i[:, :], expert_f[:, :]).then_inc(s_expert, 1)

            def tables():
                then(v.tensor_copy(half_exp_f[:, :], half_exp[:, :]))
                for e in range(E):
                    last = v.tensor_scalar(exp_of[:, e, :], expert_f[:, :], float(e),
                                           half_exp_f[:, e:e + 1], ALU.is_equal, ALU.mult)
                then(last)
                then(v.reduce_sum(exp_t[:, :], exp_of[:, :, :].rearrange("p e t -> p t e"), axis=AX.X))
                v.tensor_scalar(prod_bits[:, :], exp_t[:, :], -ONE_EXP, (SB - PK) * ONE_EXP,
                                ALU.mult, ALU.add)
                then(v.tensor_scalar(inv_bits[:, :], exp_t[:, :], ONE_EXP, (254 - SB) * ONE_EXP,
                                     ALU.mult, ALU.add))
                then(v.tensor_tensor(inv2[:, :], inv_t, inv_t, ALU.mult))
                then(v.tensor_tensor(inv3[:, :], inv2[:, :], inv_t, ALU.mult))
                dve.wait_ge(s_gates, 1)
                v.tensor_scalar(b_in[:, ER:HC], b_in[:, ER:HC], BONUS, None, ALU.add).then_inc(s_ffn_scale, 1)
                v.tensor_scalar(y_t[:, :], inv3[:, :], gates[:, 0:1], 2.0 ** PK, ALU.mult,
                                ALU.mult).then_inc(s_tables, 1)

            def ffn_scales():
                dve.wait_ge(s_ffn_sq, 5)
                then(v.reduce_sum(ffn_parts[:, 0:1], sq_parts[:, 0:3], axis=AX.X))
                then(v.tensor_scalar(ffn_parts[0:1, 0:1], ffn_parts[0:1, 0:1], 1.0, None, ALU.add))
                v.reduce_sum(ffn_parts[:, 1:2], sq_parts[:, 3:5], axis=AX.X).then_inc(s_ffn_part, 1)
                dve.wait_ge(s_ffn_tot, 1)
                then(v.tensor_copy(ffn_tot[:, :], ps_hid[:, 0:2]))
                then(v.tensor_scalar(ffn_half[:, :], ffn_tot[:, :].bitcast(i32), 24, None,
                                     ALU.logical_shift_right))
                then(v.tensor_scalar(ffn_inv_bits[:, :], ffn_half[:, :], ONE_EXP, (254 - SB) * ONE_EXP,
                                     ALU.mult, ALU.add))
                then(v.tensor_scalar(ffn_bits[:, :], ffn_half[:, :], -ONE_EXP, SB * ONE_EXP,
                                     ALU.mult, ALU.add))
                then(v.tensor_tensor(inv_both[:, :], s_ffn_inv[:, 0:1], s_ffn_inv[:, 1:2], ALU.mult))
                then(v.tensor_tensor(out_coef[:, :], inv_both[:, :], gates[:, 1:2], ALU.mult))
                v.tensor_scalar(half_inv[:, :], s_ffn_inv[:, 0:1], 0.5, None, ALU.mult)\
                 .then_inc(s_ffn_scale, 1)

            def ffn_low_parts():
                v.tensor_scalar(b_s[:, :], b_in[:, :], s_ffn[:, 0:1], None, ALU.mult)
                dve.wait_ge(s_ffn_hi, 1)
                for c in range(KC):
                    v.scalar_tensor_tensor(w_in_lo[:, c, 0:ER].rearrange("p (e r) -> p e r", r=R),
                                           wd_nat[:, :, c, :], s_ffn[:, 0:1],
                                           w_in_hi[:, c, 0:ER].rearrange("p (e r) -> p e r", r=R),
                                           ALU.mult, ALU.subtract)
                v.scalar_tensor_tensor(w_in_lo[:, :, ER:HC], wr_nat[:, :, :], s_ffn[:, 0:1],
                                       w_in_hi[:, :, ER:HC], ALU.mult, ALU.subtract)
                v.scalar_tensor_tensor(wu_lo[:, :], wu_nat[:, :], s_ffn[:, 1:2], wu_hi[:, :],
                                       ALU.mult, ALU.subtract)
                low = slice(2 * Q, 2 * Q + EF)
                v.scalar_tensor_tensor(bu3[low, :], bu_nat[low, :], s_ffn[low, 1:2], bu3[low, :],
                                       ALU.mult, ALU.subtract).then_inc(s_ffn_w, 1)

            def gate(n):
                v.memset(gate_cell[:, n:n + 1], 0.0)

            def step(i, has):
                if has(i - 1):
                    k = i - 1
                    dve.wait_ge(pT_hi_done, k + 1)
                    v.tensor_tensor(pT_lo[:, :, :], ps_pT[:, :, :], pT_hi[:, :, :],
                                    ALU.subtract).then_inc(pT_lo_done, 1)
                if has(i - 3):
                    k = i - 3
                    dve.wait_ge(tanh_done, k + 1)
                    dve.wait_ge(mix_done, k + 1)
                    wait_last(dve, wtT_done, k)
                    v.scalar_tensor_tensor(w8[:, :], half_dif[:, :], half_tanh[:, :], half_sum[:, :],
                                           ALU.mult, ALU.add).then_inc(w8_done, 1)
                    dve.wait_ge(w8_done, k + 1)
                    v.scalar_tensor_tensor(
                        weighted[:, :].rearrange("p (e r) -> p e r", r=R),
                        hid[:, 0:ER].rearrange("p (e r) -> p e r", r=R), 0.0,
                        w8[:, :].unsqueeze(2).to_broadcast([P, EF, R]), ALU.max, ALU.mult)
                    v.tensor_scalar(w_rep[:, :, 0:EF], w8[:, :].unsqueeze(1).to_broadcast([P, 3, EF]),
                                    s_ffn[:, 0:1], None, ALU.mult).then_inc(weighted_done, 1)
                if has(i + 3):
                    k = i + 3
                    dve.wait_ge(x_in, k + 1)
                    wait_last(dve, aggr1, k)
                    gate(0)
                    v.bn_stats(st1[:, :], xs[:, col(k), :].rearrange("p o d -> p (o d)")).then_inc(stats1, 1)
                    dve.wait_ge(stats1, k + 1)
                    wait_last(dve, rstd1, k)
                    gate(1)
                    v.bn_aggr(mv1[:, :], st1[:, :]).then_inc(aggr1, 1)
                if has(i):
                    k = i
                    dve.wait_ge(silu_done, k + 1)
                    v.scalar_tensor_tensor(prod[:, :], ps_a[:, :], prod_t[:, col(k)], silu[:, :],
                                           ALU.mult, ALU.mult).then_inc(prod_done, 1)
                if has(i + 1):
                    k = i + 1
                    dve.wait_ge(hT_hi_done, k + 1)
                    v.tensor_tensor(hT_lo[:, :, :], ps_hT[:, :, :], hT_hi[:, :, :],
                                    ALU.subtract).then_inc(hT_lo_done, 1)
                if has(i - 2):
                    k = i - 2
                    dve.wait_ge(h2T_hi_done, k + 1)
                    v.tensor_tensor(h2T_lo[:, :, :], ps_h2T[:, :, :], h2T_hi[:, :, :],
                                    ALU.subtract).then_inc(h2T_lo_done, 1)
                if has(i - 3):
                    k = i - 3
                    dve.wait_ge(wtT_hi_done, k + 1)
                    v.tensor_tensor(wtT_lo[:, :], ps_wT[:, 0, :], wtT_hi[:, :], ALU.subtract)
                    v.tensor_tensor(gwT[Q:Q + EF, :], ps_wT[Q:Q + EF, 1, :], gwT[Q:Q + EF, :],
                                    ALU.subtract).then_inc(wtT_lo_done, 1)
                if has(i - 1):
                    k = i - 1
                    row = xs[:, col(k), :].rearrange("p o d -> p (o d)")
                    dve.wait_ge(y_done, k + 1)
                    v.scalar_tensor_tensor(row, ps_y[:, :], y_t[:, col(k)], row,
                                           ALU.mult, ALU.add).then_inc(x1_done, 1)
                    dve.wait_ge(x1_done, k + 1)
                    wait_last(dve, aggr2, k)
                    gate(2)
                    v.bn_stats(st2[:, :], row).then_inc(stats2, 1)
                    dve.wait_ge(stats2, k + 1)
                    wait_last(dve, rstd2, k)
                    gate(3)
                    v.bn_aggr(mv2[:, :], st2[:, :]).then_inc(aggr2, 1)
                if has(i - 2):
                    k = i - 2
                    dve.wait_ge(hid_mm, k + 1)
                    wait_last(dve, weighted_done, k)
                    v.tensor_tensor(hid[:, :], ps_hid[:, 0:HC], b_s[:, :], ALU.add).then_inc(hid_done, 1)
                    dve.wait_ge(hid_done, k + 1)
                    gate(4)
                    v.max(top8[:, :], hid[:, ER:HC]).then_inc(top_done, 1)
                    dve.wait_ge(top_done, k + 1)
                    v.tensor_tensor(gap[:, :], top8[:, 0:1], top8[:, 1:2], ALU.subtract).then_inc(gap_done, 1)
                    v.max_index(arg8[:, :], top8[:, :], hid[:, ER:HC]).then_inc(arg_done, 1)
                    dve.wait_ge(arg_done, k + 1)
                    v.tensor_copy(arg8f[:, :], arg8[:, :]).then_inc(argf_done, 1)
                    dve.wait_ge(argf_done, k + 1)
                    v.tensor_scalar(half_first[:, :], slot_no[:, 0:EF], arg8f[:, 0:1], 0.5,
                                    ALU.is_equal, ALU.mult)
                    v.tensor_scalar(half_second[:, :], slot_no[:, 0:EF], arg8f[:, 1:2], 0.5,
                                    ALU.is_equal, ALU.mult).then_inc(halves_done, 1)
                    dve.wait_ge(halves_done, k + 1)
                    v.tensor_tensor(half_sum[:, :], half_first[:, :], half_second[:, :], ALU.add)
                    v.tensor_tensor(half_dif[:, :], half_first[:, :], half_second[:, :],
                                    ALU.subtract).then_inc(mix_done, 1)
                if has(i - 3):
                    k = i - 3
                    row = xs[:, col(k), :].rearrange("p o d -> p (o d)")
                    dve.wait_ge(o_mm, k + 1)
                    v.scalar_tensor_tensor(row, ps_o[:, :], out_coef[:, :], row,
                                           ALU.mult, ALU.add).then_inc(out_done, 1)

            row_numbers()
            top_rows(0)
            experts()
            scales(0)
            top_rows(1)
            low_parts(0)
            scales(1)
            step(-3, some)
            square_sums(2)
            square_sums(3)
            top_rows(2)
            low_parts(1, range(0, 2))
            scales(2)
            low_parts(1, range(2, KC))
            step(-2, some)
            low_parts(2)
            step(-1, some)
            low_parts(3)
            tables()
            step(0, some)
            ffn_scales()
            ffn_low_parts()
            pipeline(dve, step, 1)


_INS = ['x', 'itok_BxS_13_99985', 'ctx_2048', 'g_xattn', 'g_ffn', 'L0_ffn_Wr', 'L0_ffn_br',
        'L0_ffn_Wd', 'L0_ffn_bd', 'L0_ffn_Wu', 'L0_ffn_bu']
_OUTS = [((4, 512, 512), 'float32')]


def kernel(**inputs):
    import numpy as _np
    import concourse.bacc as _bacc
    from concourse import mybir as _mybir
    from concourse.bass_utils import run_bass_kernel_spmd as _run

    nc = _bacc.Bacc("TRN2", target_bir_lowering=False, num_devices=1)
    arrays, args = {}, []
    for name in _INS:
        a = _np.ascontiguousarray(inputs[name])
        arrays[f"in_{name}_dram"] = a
        args.append(nc.dram_tensor(f"in_{name}_dram", a.shape, _mybir.dt.from_np(a.dtype), kind="ExternalInput").ap())
    for i, (shape, dtype) in enumerate(_OUTS):
        dt = _mybir.dt.from_np(_np.dtype(dtype))
        args.append(nc.dram_tensor(f"out_{i}_dram", shape, dt, kind="ExternalOutput").ap())
    bass_flamingo_gated_kernel(nc, *args)
    r = _run(nc, [arrays], core_ids=[0])
    got = tuple(r.results[0][f"out_{i}_dram"] for i in range(len(_OUTS)))
    return got[0]
```

```python
import numpy as np
import concourse.bass as bass
from concourse import mybir
from contextlib import ExitStack


def bass_flamingo_gated_kernel(
    nc: bass.Bass,
    x: bass.AP,
    tok: bass.AP,
    ctx_w: bass.AP,
    g_xattn: bass.AP,
    g_ffn: bass.AP,
    Wr: bass.AP,
    br: bass.AP,
    Wd: bass.AP,
    bd: bass.AP,
    Wu: bass.AP,
    bu: bass.AP,
    out: bass.AP,
):
    fp32, fp16 = mybir.dt.float32, mybir.dt.float16
    i32, u32 = mybir.dt.int32, mybir.dt.uint32
    ALU = mybir.AluOpType
    ACT = mybir.ActivationFunctionType
    AX = mybir.AxisListType

    P = 128
    B, S, D = x.shape
    N = B * S
    E = ctx_w.shape[0]
    KC = D // P
    C = N // P
    T = N // P
    NP = T + E - 1
    LATE = E - 1
    VOCAB = 25000
    PER_EXPERT = VOCAB // E
    EF, _, R = Wd.shape
    ER = EF * R
    HC = ER + EF
    BONUS = 3.0 * (1.0 - min(1 / 1250, 1.0))
    EPS = 1e-5

    WK = 10
    PK = 15
    SB = 127 + 63 + WK
    ONE_EXP = float(1 << 23)

    x_rows = x.rearrange("b s d -> (b s) d")
    out_rows = out.rearrange("b s d -> (b s) d")

    ctx = ExitStack()
    with ctx:
        def sb(name, shape, dt=fp32):
            return ctx.enter_context(nc.sbuf_tensor(name, shape, dt))

        def pb(name, shape, dt=fp32):
            return ctx.enter_context(nc.psum_tensor(name, shape, dt))

        def sem(name):
            return ctx.enter_context(nc.semaphore(name))

        ident = sb("ident", [P, P])
        before = sb("before", [P, P])
        ones = sb("ones", [P, P])
        slot_no = sb("slot_no", [P, P])
        slot_no16 = sb("slot_no16", [P, P], fp16)
        pair_no = sb("pair_no", [P, NP])
        row_id1 = sb("row_id1", [P, C])

        tok_i = sb("tok_i", [P, C], i32)
        ge = sb("ge", [P, E + 1, C])
        member = sb("member", [P, E, C])
        zeros = sb("zeros", [P, E * C])
        run = sb("run", [P, E * C])
        per_row = sb("per_row", [P, E])
        prev_end = sb("prev_end", [P, E])
        token_e = sb("token_e", [P, C])
        end_slot = sb("end_slot", [P, E])
        shift = sb("shift", [P, E])
        cand = sb("cand", [P, E, C])
        slot1 = sb("slot1", [P, C])
        slot_i = sb("slot_i", [P, C], i32)
        tile_i = sb("tile_i", [P, C], i32)
        in_tile_i = sb("in_tile_i", [P, C], i32)
        tile_f = sb("tile_f", [P, C])
        pair_f = sb("pair_f", [P, C])
        in_tile_f = sb("in_tile_f", [P, C], fp16)
        in_tile_f32 = sb("in_tile_f32", [P, C])
        hot_slot = sb("hot_slot", [P, C, P], fp16)
        is_tile = sb("is_tile", [P, C, T])
        hot_tile = sb("hot_tile", [P, C, T], fp16)
        hot_pair = sb("hot_pair", [P, C, NP], fp16)
        rows_of = sb("rows_of", [P, T], u32)
        in_pair = sb("in_pair", [P, NP])
        start_i = sb("start_i", [P, E - 1], i32)
        start_f = sb("start_f", [P, E - 1])
        first_pair = sb("first_pair", [P, E - 1])
        past = sb("past", [P, E - 1, NP])
        expert_f = sb("expert_f", [P, NP])
        expert_i = sb("expert_i", [P, NP], i32)
        pair_tile = sb("pair_tile", [P, NP])
        pair_tile_i = sb("pair_tile_i", [P, NP], i32)
        new_tile = sb("new_tile", [P, NP])
        again = sb("again", [P, NP])
        source_f = sb("source_f", [P, NP])
        source_i = sb("source_i", [P, NP], i32)

        w_nat = sb("w_nat", [P, E, KC, D])
        w_hi = sb("w_hi", [P, E, KC, D], fp16)
        w_lo = sb("w_lo", [P, E, KC, D], fp16)
        w_full = sb("w_full", [P, KC, D])
        sq_act = sb("sq_act", [P, D])
        row_sq = sb("row_sq", [P, E, KC])
        part_sq = sb("part_sq", [P, E])
        top_sq = sb("top_sq", [1, E])
        top_all = sb("top_all", [P, E])
        half_exp = sb("half_exp", [P, E], i32)
        half_exp_f = sb("half_exp_f", [P, E])
        scale_w = sb("scale_w", [P, E], i32)
        s_w = scale_w[:, :].bitcast(fp32)
        exp_of = sb("exp_of", [P, E, NP])
        exp_t = sb("exp_t", [P, NP])
        inv_bits = sb("inv_bits", [P, NP], i32)
        prod_bits = sb("prod_bits", [P, NP], i32)
        inv_t = inv_bits[:, :].bitcast(fp32)
        prod_t = prod_bits[:, :].bitcast(fp32)
        inv2 = sb("inv2", [P, NP])
        inv3 = sb("inv3", [P, NP])
        y_all = sb("y_all", [P, NP])
        y_t = sb("y_t", [P, NP])
        gates_in = sb("gates_in", [P, 2])
        gates = sb("gates", [P, 2])

        wd_nat = sb("wd_nat", [P, EF, KC, R])
        wr_nat = sb("wr_nat", [P, KC, EF])
        w_in_hi = sb("w_in_hi", [P, KC, HC], fp16)
        w_in_lo = sb("w_in_lo", [P, KC, HC], fp16)
        b_in = sb("b_in", [P, HC])
        b_s = sb("b_s", [P, HC])
        wu_nat = sb("wu_nat", [ER, D])
        wu_hi = sb("wu_hi", [ER, D], fp16)
        wu_lo = sb("wu_lo", [ER, D], fp16)
        Q = 32
        Q3 = 3 * Q
        bu_nat = sb("bu_nat", [Q3, D])
        bu3 = sb("bu3", [Q3, D], fp16)
        sq_parts = sb("sq_parts", [P, 5])
        ffn_parts = sb("ffn_parts", [P, 2])
        ffn_tot = sb("ffn_tot", [P, 2])
        ffn_half = sb("ffn_half", [P, 2], i32)
        ffn_bits = sb("ffn_bits", [P, 2], i32)
        ffn_inv_bits = sb("ffn_inv_bits", [P, 2], i32)
        s_ffn = ffn_bits[:, :].bitcast(fp32)
        s_ffn_inv = ffn_inv_bits[:, :].bitcast(fp32)
        half_inv = sb("half_inv", [P, 1])
        inv_both = sb("inv_both", [P, 1])
        out_coef = sb("out_coef", [P, 1])

        xs = sb("xs", [P, 2 * T, D])
        x1 = xs[:, T:2 * T, :]
        st1 = sb("st1", [P, 6])
        mv1 = sb("mv1", [P, 2])
        st2 = sb("st2", [P, 6])
        mv2 = sb("mv2", [P, 2])
        ve = sb("ve", [P, 2, T])
        rs = sb("rs", [P, 2, T])
        mrs = sb("mrs", [P, 2, T])
        neg_half = sb("neg_half", [P, 1])
        h = sb("h", [P, D])
        hT_hi = sb("hT_hi", [P, KC, P], fp16)
        hT_lo = sb("hT_lo", [P, KC, P], fp16)
        silu = sb("silu", [P, D])
        prod = sb("prod", [P, D])
        pT_hi = sb("pT_hi", [P, KC, P], fp16)
        pT_lo = sb("pT_lo", [P, KC, P], fp16)
        h2 = sb("h2", [P, KC, P])
        h2T_hi = sb("h2T_hi", [P, KC, P], fp16)
        h2T_lo = sb("h2T_lo", [P, KC, P], fp16)
        hid = sb("hid", [P, HC])
        top8 = sb("top8", [P, 8])
        arg8 = sb("arg8", [P, 8], u32)
        arg8f = sb("arg8f", [P, 8])
        gate_cell = sb("gate_cell", [P, 5])
        gap = sb("gap", [P, 1])
        half_tanh = sb("half_tanh", [P, 1])
        half_first = sb("half_first", [P, EF])
        half_second = sb("half_second", [P, EF])
        half_sum = sb("half_sum", [P, EF])
        half_dif = sb("half_dif", [P, EF])
        w8 = sb("w8", [P, EF])
        weighted = sb("weighted", [P, ER])
        w_rep = sb("w_rep", [P, 3, Q])
        wtT_hi = sb("wtT_hi", [P, P], fp16)
        wtT_lo = sb("wtT_lo", [P, P], fp16)
        gwT = sb("gwT", [Q3, P], fp16)

        ps_hT = pb("ps_hT", [P, KC, P])
        ps_a = pb("ps_a", [P, D])
        ps_pT = pb("ps_pT", [P, KC, P])
        ps_y = pb("ps_y", [P, D])
        ps_h2T = pb("ps_h2T", [P, KC, P])
        ps_hid = pb("ps_hid", [P, D])
        ps_wT = pb("ps_wT", [P, KC, P])
        ps_o = pb("ps_o", [P, D])

        s_tok = sem("s_tok")
        s_wload = [sem(f"s_wload{e}") for e in range(E)]
        s_small = sem("s_small")
        s_gather = [sem(f"s_gather{t}") for t in range(T)]
        s_scatter = sem("s_scatter")
        s_const = sem("s_const")
        s_pool = sem("s_pool")
        s_route = sem("s_route")
        s_counts = sem("s_counts")
        s_rows_mm = sem("s_rows_mm")
        s_in_tile = sem("s_in_tile")
        s_hot = sem("s_hot")
        s_hot_pool = sem("s_hot_pool")
        s_gather_rows = sem("s_gather_rows")
        s_hot_pair = sem("s_hot_pair")
        s_expert_f = sem("s_expert_f")
        s_expert = sem("s_expert")
        s_places = sem("s_places")
        s_sq = sem("s_sq")
        s_partsq = sem("s_partsq")
        s_sqT = sem("s_sqT")
        s_topsq = sem("s_topsq")
        s_topall = sem("s_topall")
        s_scale = sem("s_scale")
        s_gates_in = sem("s_gates_in")
        s_gates = sem("s_gates")
        s_tables = sem("s_tables")
        s_y_t = sem("s_y_t")
        s_wT = sem("s_wT")
        s_whi = sem("s_whi")
        s_wlo = sem("s_wlo")
        s_wlo_pool = sem("s_wlo_pool")
        s_ffn_sq = sem("s_ffn_sq")
        s_ffn_part = sem("s_ffn_part")
        s_ffn_tot = sem("s_ffn_tot")
        s_ffn_scale = sem("s_ffn_scale")
        s_ffn_hi = sem("s_ffn_hi")
        s_ffn_w = sem("s_ffn_w")
        x_in = sem("x_in")
        stats1 = sem("stats1")
        aggr1 = sem("aggr1")
        rstd1 = sem("rstd1")
        normed1 = sem("normed1")
        hT_done = sem("hT_done")
        hT_hi_done = sem("hT_hi_done")
        hT_lo_done = sem("hT_lo_done")
        a_done = sem("a_done")
        silu_done = sem("silu_done")
        prod_done = sem("prod_done")
        pT_done = sem("pT_done")
        pT_hi_done = sem("pT_hi_done")
        pT_lo_done = sem("pT_lo_done")
        y_done = sem("y_done")
        x1_done = sem("x1_done")
        stats2 = sem("stats2")
        aggr2 = sem("aggr2")
        rstd2 = sem("rstd2")
        rs_step = sem("rs_step")
        normed2 = sem("normed2")
        h2T_done = sem("h2T_done")
        h2T_hi_done = sem("h2T_hi_done")
        h2T_lo_done = sem("h2T_lo_done")
        hid_mm = sem("hid_mm")
        hid_done = sem("hid_done")
        top_done = sem("top_done")
        arg_done = sem("arg_done")
        gap_done = sem("gap_done")
        tanh_done = sem("tanh_done")
        mix_done = sem("mix_done")
        w8_done = sem("w8_done")
        weighted_done = sem("weighted_done")
        wtT_done = sem("wtT_done")
        wtT_hi_done = sem("wtT_hi_done")
        wtT_lo_done = sem("wtT_lo_done")
        o_mm = sem("o_mm")
        out_done = sem("out_done")

        block = ctx.enter_context(nc.Block())

        def some(n, off, i):
            return 0 <= i + off < n

        def pipeline(eng, step, first, pairs, tiles):
            def work(i):
                return ([(some(NP, off, i), i + off == 0) for off in pairs]
                        + [(some(T, off, i), i + off == 0) for off in tiles])

            end = max(NP - min(pairs), T - min(tiles))
            while first < end:
                last = first + 1
                while last < end and work(last) == work(first):
                    last += 1
                if last == first + 1:
                    step(first, first)
                else:
                    odd = (last - first) % 2
                    if odd:
                        step(first, first)
                    with eng.Fori(0, (last - first) // 2) as n:
                        step(n * 2 + (first + odd), first)
                        step(n * 2 + (first + odd + 1), first)
                first = last

        def col(k):
            return bass.ds(k, 1)

        def flat(row):
            return row.rearrange("p o d -> p (o d)")

        def wait_last(eng, done, k):
            if not (isinstance(k, int) and k == 0):
                eng.wait_ge(done, k)

        AHEAD = 4
        w_banks = [[ps_pT, ps_y, ps_wT, ps_o], [ps_h2T, ps_pT, ps_y, ps_wT],
                   [ps_o, ps_y, ps_h2T, ps_wT], [ps_h2T, ps_wT, ps_o, ps_hid]]

        def w_bank(e, kc):
            bank = w_banks[e][kc]
            return bank[:, :, :].rearrange("p c q -> p (c q)") if len(bank.shape) == 3 else bank[:, :]

        DVE_HOT = 3 * C // 4
        DVE_LOW = [KC, KC] + [KC - 1] * (E - 2)

        def low_done(e, kc):
            if kc < DVE_LOW[e]:
                return s_wlo, sum(DVE_LOW[:e]) + kc + 1
            return s_wlo_pool, sum(KC - n for n in DVE_LOW[:e]) + kc - DVE_LOW[e] + 1

        def wait_low(eng, e):
            for kc in (DVE_LOW[e] - 1, KC - 1):
                eng.wait_ge(*low_done(e, kc))

        def last_in_bank(e, kc):
            before_it = [divmod(n, KC) for n in range(e * KC + kc)
                         if w_banks[n // KC][n % KC] is w_banks[e][kc]]
            return before_it[-1] if before_it else None

        @block.sync
        def _(sp):
            def load_weights(e):
                sp.dma_start(w_nat[:, e, :, :], ctx_w[e, :, :].rearrange("(c p) k -> p c k", p=P))\
                  .then_inc(s_wload[e], 16)

            sp.dma_start(tok_i[:, :], tok.rearrange("b (q c) -> (b q) c", c=C)).then_inc(s_tok, 16)
            load_weights(0)
            load_weights(1)
            load_weights(2)
            for t in range(T):
                sp.wait_ge(s_gather[t], 16)
                sp.sem_inc(x_in, 1)
                if t == 0:
                    load_weights(3)
                if t == 1:
                    sp.dma_start(gates_in[:, 0:1],
                                 g_xattn.rearrange("(a n) -> a n", a=1).to_broadcast([P, 1])).then_inc(s_gates_in, 16)
                    sp.dma_start(gates_in[:, 1:2],
                                 g_ffn.rearrange("(a n) -> a n", a=1).to_broadcast([P, 1])).then_inc(s_gates_in, 16)
                if t == AHEAD - 1:
                    sp.dma_start(b_in[:, 0:ER],
                                 bd.rearrange("(a e) r -> a (e r)", a=1).to_broadcast([P, ER])).then_inc(s_small, 16)
                    sp.dma_start(b_in[:, ER:HC],
                                 br.rearrange("(a e) -> a e", a=1).to_broadcast([P, EF])).then_inc(s_small, 16)
                    sp.dma_start(wr_nat[:, :, :],
                                 Wr.rearrange("(p c) e -> p c e", c=KC)).then_inc(s_small, 16)
                    sp.dma_start(wd_nat[:, :, :, :],
                                 Wd.rearrange("e (p c) r -> p e (c r)", c=KC)).then_inc(s_small, 16)
                    sp.dma_start(wu_nat[:, :], Wu.rearrange("e r d -> (e r) d")).then_inc(s_small, 16)
                    sp.wait_ge(s_const, 2)
                    for n in range(3):
                        sp.dma_start(bu_nat[n * Q:n * Q + EF, :], bu[:, :]).then_inc(s_small, 16)
            sp.wait_ge(s_scatter, 16 * T)

        @block.gpsimd
        def _(pool):
            g = nc.gpsimd
            g.memset(neg_half[:, :], -0.5).then_inc(s_pool, 1)
            g.memset(before[:, :], 1.0).then_inc(s_pool, 1)
            g.memset(ident[:, :], 0.0).then_inc(s_pool, 1)
            g.memset(ones[:, :], 1.0)
            pool.wait_ge(s_pool, 3)
            g.affine_select(out=ident[:, :], in_=ident[:, :], compare_op=ALU.not_equal, fill=1.0,
                            base=0, pattern=[[-1, P]], channel_multiplier=1)
            g.affine_select(out=before[:, :], in_=before[:, :], compare_op=ALU.is_gt, fill=0.0,
                            base=0, pattern=[[1, P]], channel_multiplier=-1)
            g.iota(row_id1[:, :], pattern=[[1, C]], base=1, channel_multiplier=C,
                   allow_small_or_imprecise_dtypes=True)
            g.iota(pair_no[:, :], pattern=[[1, NP]], base=0, channel_multiplier=0,
                   allow_small_or_imprecise_dtypes=True)
            g.iota(slot_no[:, :], pattern=[[1, P]], base=0, channel_multiplier=0,
                   allow_small_or_imprecise_dtypes=True).then_inc(s_const, 1)
            g.memset(bu_nat[:, :], 0.0)
            g.memset(w_rep[:, :, :], 0.0)
            g.memset(new_tile[:, 0:1], 1.0)
            g.memset(sq_parts[:, :], 0.0).then_inc(s_const, 1)
            pool.wait_ge(s_in_tile, 1)
            for c in range(DVE_HOT, C):
                last = g.tensor_scalar(hot_slot[:, c, :], slot_no[:, :], in_tile_f32[:, c:c + 1], None,
                                       ALU.is_equal)
            last.then_inc(s_hot_pool, 1)
            pool.wait_ge(s_gather_rows, 1)

            def gather(t):
                if t < T:
                    g.indirect_dma_start(
                        out=xs[:, t, :], out_offset=None, in_=x_rows[:, :],
                        in_offset=bass.IndirectOffsetOnAxis(ap=rows_of[:, t:t + 1], axis=0),
                    ).then_inc(s_gather[t], 16)

            for t in range(AHEAD):
                gather(t)
            steps = [0]

            def then(ins):
                steps[0] += 1
                ins.then_inc(rs_step, 1)
                pool.wait_ge(rs_step, steps[0])

            def rstd(n, mv, k, done):
                then(g.tensor_scalar(ve[:, n, k:k + 1], mv[:, 1:2], EPS, None, ALU.add))
                then(g.tensor_tensor(rs[:, n, k:k + 1], ve[:, n, k:k + 1], neg_half[:, :], ALU.pow))
                g.tensor_scalar(mrs[:, n, k:k + 1], mv[:, 0:1], -1.0, rs[:, n, k:k + 1],
                                ALU.mult, ALU.mult).then_inc(done, 1)

            def pairs_tiles():
                pool.wait_ge(s_expert_f, 1)
                then(g.tensor_tensor(pair_tile[:, :], pair_no[:, :], expert_f[:, :], ALU.subtract))
                then(g.tensor_scalar(pair_tile[:, :], pair_tile[:, :], float(T - 1), None, ALU.min))
                g.tensor_copy(pair_tile_i[:, :], pair_tile[:, :])
                then(g.tensor_tensor(new_tile[:, 1:NP], pair_tile[:, 1:NP], pair_tile[:, 0:NP - 1],
                                     ALU.subtract))
                then(g.tensor_scalar(again[:, :], new_tile[:, :], -float(T), float(T), ALU.mult, ALU.add))
                then(g.tensor_tensor(source_f[:, :], again[:, :], pair_tile[:, :], ALU.add))
                g.tensor_copy(source_i[:, :], source_f[:, :]).then_inc(s_places, 1)

            def y_factors(n, p0, p1):
                cols = slice(p0, p1)
                pool.wait_ge(s_tables, n)
                pool.wait_ge(s_expert, 1)
                pool.wait_ge(s_gates, 1)
                then(g.tensor_tensor(inv2[:, cols], inv_t[:, cols], inv_t[:, cols], ALU.mult))
                then(g.tensor_tensor(inv3[:, cols], inv2[:, cols], inv_t[:, cols], ALU.mult))
                then(g.tensor_scalar(y_all[:, cols], inv3[:, cols], gates[:, 0:1], 2.0 ** PK,
                                     ALU.mult, ALU.mult))
                g.tensor_tensor(y_t[:, cols], y_all[:, cols], in_pair[:, cols],
                                ALU.mult).then_inc(s_y_t, 1)

            def choice(k):
                pool.wait_ge(arg_done, k + 1)
                then(g.tensor_copy(arg8f[:, :], arg8[:, :]))
                if k:
                    pool.wait_ge(w8_done, k)
                g.tensor_scalar(half_first[:, :], slot_no[:, 0:EF], arg8f[:, 0:1], 0.5,
                                  ALU.is_equal, ALU.mult)
                then(g.tensor_scalar(half_second[:, :], slot_no[:, 0:EF], arg8f[:, 1:2], 0.5,
                                       ALU.is_equal, ALU.mult))
                g.tensor_tensor(half_sum[:, :], half_first[:, :], half_second[:, :], ALU.add)
                g.tensor_tensor(half_dif[:, :], half_first[:, :], half_second[:, :],
                                  ALU.subtract).then_inc(mix_done, 1)

            def low_part(e):
                for kc in range(DVE_LOW[e], KC):
                    pool.wait_ge(s_whi, e * KC + kc + 1)
                    g.tensor_tensor(w_lo[:, e, kc, :], w_full[:, kc, :], w_hi[:, e, kc, :],
                                    ALU.subtract).then_inc(s_wlo_pool, 1)

            for i in range(-3, T + LATE + 5):
                k = i - 3 - LATE
                if 0 <= k < T:
                    choice(k)
                if i == 0:
                    y_factors(1, 0, 2)
                if 0 < i + 1 < E:
                    low_part(i + 1)
                if i == 2:
                    y_factors(2, 2, NP)
                if some(T, 3, i):
                    pool.wait_ge(aggr1, i + 4)
                    rstd(0, mv1, i + 3, rstd1)
                if i == -3:
                    pairs_tiles()
                gather(i + 3 + AHEAD)
                k = i - 5 - LATE
                if 0 <= k < T:
                    pool.wait_ge(out_done, k + 1)
                    g.indirect_dma_start(
                        out=out_rows[:, :],
                        out_offset=bass.IndirectOffsetOnAxis(ap=rows_of[:, k:k + 1], axis=0),
                        in_=x1[:, k, :], in_offset=None,
                    ).then_inc(s_scatter, 16)
                k = i - 1 - LATE
                if 0 <= k < T:
                    pool.wait_ge(aggr2, k + 1)
                    rstd(1, mv2, k, rstd2)

        @block.tensor
        def _(pe):
            mm, tr = nc.tensor.matmul, nc.tensor.transpose

            def w_blocks(e, blocks=range(KC)):
                pe.wait_ge(s_wload[e], 16)
                for kc in blocks:
                    if last_in_bank(e, kc):
                        pe.wait_ge(*low_done(*last_in_bank(e, kc)))
                    for c in range(KC):
                        last = tr(w_bank(e, kc)[:, c * P:(c + 1) * P],
                                  w_nat[:, e, c, kc * P:(kc + 1) * P], ident[:, :])
                    last.then_inc(s_wT, 1)

            def top_norms_T(e):
                pe.wait_ge(s_partsq, e + 1)
                if e:
                    pe.wait_ge(s_scale, e)
                tr(ps_hid[0:1, 0:P], part_sq[:, e:e + 1], ident[:, :]).then_inc(s_sqT, 1)

            def top_norm(e):
                pe.wait_ge(s_topsq, e + 1)
                mm(ps_hid[:, P:P + 1], ones[0:1, :], top_sq[:, e:e + 1],
                   start=True, stop=True).then_inc(s_topall, 1)

            pe.wait_ge(s_const, 1)
            pe.wait_ge(s_counts, 1)
            mm(ps_hid[:, 0:E], before[:, :], per_row[:, :], start=True, stop=True)
            mm(ps_hid[:, E:2 * E], ones[:, :], per_row[:, :], start=True, stop=True).then_inc(s_rows_mm, 1)
            w_blocks(0)
            pe.wait_ge(s_hot, 1)
            for c in range(C):
                if c == C // 2:
                    pe.wait_ge(s_hot, 2)
                if c == DVE_HOT:
                    pe.wait_ge(s_hot_pool, 1)
                last = mm(ps_hT[:, 0, 0:T], hot_slot[:, c, :], hot_tile[:, c, :],
                          start=(c == 0), stop=(c == C - 1))
                if c == C // 2 - 1:
                    top_norms_T(0)
            last.then_inc(s_rows_mm, 1)
            top_norm(0)
            pe.wait_ge(s_hot_pair, 1)
            for c in range(C):
                last = mm(ps_a[:, 0:NP], hot_slot[:, c, :], hot_pair[:, c, :],
                          start=(c == 0), stop=(c == C - 1))
            last.then_inc(s_rows_mm, 1)
            w_blocks(1, range(0, 1))
            top_norms_T(1)
            top_norm(1)
            w_blocks(1, range(1, 3))

            def split_product(ps, lhs_hi, lhs_lo, e):
                for kc in range(KC):
                    hi = w_hi[:, bass.ds(e, 1), kc, :].rearrange("p e n -> p (e n)")
                    lo = w_lo[:, bass.ds(e, 1), kc, :].rearrange("p e n -> p (e n)")
                    mm(ps[:, :], lhs_hi[:, kc, :], hi, start=(kc == 0), stop=False)
                    mm(ps[:, :], lhs_hi[:, kc, :], lo, start=False, stop=False)
                    last = mm(ps[:, :], lhs_lo[:, kc, :], hi, start=False, stop=(kc == KC - 1))
                return last

            def expert_of(k):
                return pe.value_load(expert_i[0:1, col(k)], min_val=0, max_val=E - 1)

            def second_product(k, e):
                pe.wait_ge(pT_lo_done, k + 1)
                wait_last(pe, x1_done, k)
                if isinstance(k, int) and k == 0:
                    pe.wait_ge(*low_done(2, w_banks[2].index(ps_y)))
                split_product(ps_y, pT_hi, pT_lo, e).then_inc(y_done, 1)

            def transpose_product(k):
                pe.wait_ge(prod_done, k + 1)
                for c in range(KC):
                    last = tr(ps_pT[:, c, :], prod[:, c * P:(c + 1) * P], ident[:, :])
                last.then_inc(pT_done, 1)

            def hidden_product(k):
                pe.wait_ge(h2T_lo_done, k + 1)
                wait_last(pe, hid_done, k)
                for c in range(KC):
                    mm(ps_hid[:, 0:HC], h2T_hi[:, c, :], w_in_hi[:, c, :], start=(c == 0), stop=False)
                    mm(ps_hid[:, 0:HC], h2T_hi[:, c, :], w_in_lo[:, c, :], start=False, stop=False)
                    last = mm(ps_hid[:, 0:HC], h2T_lo[:, c, :], w_in_hi[:, c, :],
                              start=False, stop=(c == KC - 1))
                last.then_inc(hid_mm, 1)

            def low_rank_out(k):
                pe.wait_ge(wtT_lo_done, k + 1)
                wait_last(pe, out_done, k)
                mm(ps_o[:, :], wtT_hi[:, :], wu_hi[:, :], start=True, stop=False)
                mm(ps_o[:, :], wtT_hi[:, :], wu_lo[:, :], start=False, stop=False)
                mm(ps_o[:, :], wtT_lo[:, :], wu_hi[:, :], start=False, stop=False)
                mm(ps_o[:, :], gwT[:, :], bu3[:, :], start=False, stop=True).then_inc(o_mm, 1)

            def experts_of(i, i0):
                return (expert_of(i - 1) if some(NP, -1, i0) else None,
                        expert_of(i) if some(NP, 0, i0) else None)

            def step(i, i0, experts=None, meanwhile=None):
                has_y, has_a = some(NP, -1, i0), some(NP, 0, i0)
                e_last, e_now = experts or experts_of(i, i0)
                if has_y and not has_a:
                    transpose_product(i - 1)
                if some(T, -3 - LATE, i0) and (has_y or some(NP, -2, i0)):
                    hidden_product(i - 3 - LATE)
                if has_y and has_a:
                    transpose_product(i - 1)
                if some(NP, 0, i0):
                    k = i
                    if isinstance(i, int) and i < E:
                        wait_low(pe, i)
                    pe.wait_ge(hT_lo_done, k + 1)
                    split_product(ps_a, hT_hi, hT_lo, e_now).then_inc(a_done, 1)
                if some(T, -4 - LATE, i0) and has_a:
                    low_rank_out(i - 4 - LATE)
                if meanwhile:
                    meanwhile()
                if some(NP, 1, i0):
                    k = i + 1
                    pe.wait_ge(normed1, k + 1)
                    for c in range(KC):
                        last = tr(ps_hT[:, c, :], h[:, c * P:(c + 1) * P], ident[:, :])
                    last.then_inc(hT_done, 1)
                if has_y and not has_a:
                    second_product(i - 1, e_last)
                if some(T, -2 - LATE, i0):
                    k = i - 2 - LATE
                    pe.wait_ge(normed2, k + 1)
                    for c in range(KC):
                        last = tr(ps_h2T[:, c, :], h2[:, c, :], ident[:, :])
                    last.then_inc(h2T_done, 1)
                if some(T, -4 - LATE, i0) and not has_a:
                    low_rank_out(i - 4 - LATE)
                if some(T, -2 - LATE, i0) and not has_y:
                    hidden_product(i - 2 - LATE)
                if has_y and has_a:
                    second_product(i - 1, e_last)
                if some(T, -3 - LATE, i0):
                    k = i - 3 - LATE
                    pe.wait_ge(weighted_done, k + 1)
                    wait_last(pe, wtT_lo_done, k)
                    tr(ps_wT[:, 0, :], weighted[:, :], ident[:, :])
                    tr(ps_wT[0:Q3, 1, :], w_rep[:, :, :].rearrange("p a q -> p (a q)"),
                       ident[:, :]).then_inc(wtT_done, 1)

            step(-1, -1)
            w_blocks(1, range(3, KC))
            pe.wait_ge(s_expert, 1)
            experts_0 = experts_of(0, 0)
            top_norms_T(2)
            step(0, 0, experts_0, meanwhile=lambda: top_norm(2))
            w_blocks(2)
            step(1, 1)
            experts_2 = experts_of(2, 2)
            w_blocks(3, range(0, KC - 1))
            top_norms_T(3)
            top_norm(3)

            def rest_of_w3():
                pe.wait_ge(s_scale, E)
                w_blocks(3, range(KC - 1, KC))

            step(2, 2, experts_2, meanwhile=rest_of_w3)
            step(3, 3)
            pe.wait_ge(s_ffn_part, 1)
            mm(ps_hid[:, 0:2], ones[:, :], ffn_parts[:, :], start=True, stop=True).then_inc(s_ffn_tot, 1)
            step(4, 4)
            step(5, 5)
            pe.wait_ge(s_ffn_w, 1)
            step(6, 6)
            pe.wait_ge(s_ffn_w, 2)
            pipeline(pe, step, 7, (-1, 0, 1), (-2 - LATE, -3 - LATE, -4 - LATE))

        @block.scalar
        def _(act):
            a = nc.scalar.activation

            def square_sums(e, blocks=range(KC)):
                act.wait_ge(s_wload[e], 16)
                for c in blocks:
                    act.wait_ge(s_sq, 1 + e * KC + c)
                    a(sq_act[:, :], w_nat[:, e, c, :], ACT.Square,
                      accum_out=row_sq[:, e, c:c + 1]).then_inc(s_sq, 1)

            def high_parts(e, blocks=range(KC)):
                act.wait_ge(s_scale, e + 1)
                for kc in blocks:
                    act.wait_ge(s_wT, e * KC + kc + 1)
                    if kc >= DVE_LOW[e]:
                        if e > 1 and kc >= DVE_LOW[e - 1]:
                            act.wait_ge(*low_done(e - 1, kc))
                        a(w_full[:, kc, :], w_bank(e, kc), ACT.Copy, scale=s_w[:, e:e + 1])
                    a(w_hi[:, e, kc, :], w_bank(e, kc), ACT.Copy, scale=s_w[:, e:e + 1]).then_inc(s_whi, 1)

            def ffn_squares():
                act.wait_ge(s_small, 16 * 8)
                act.wait_ge(s_sq, 1 + E * KC)
                parts = [(wd_nat[:, :, :, :], sq_act[:, :].rearrange("p (e c r) -> p e c r", c=KC, r=R), P),
                         (wr_nat[:, :, :], sq_act[:, 0:KC * EF].rearrange("p (c e) -> p c e", e=EF), P),
                         (b_in[0:1, :], sq_act[0:1, 0:HC], 1),
                         (wu_nat[:, :], sq_act[:, :], ER),
                         (bu_nat[0:EF, :], sq_act[0:EF, :], EF)]
                act.wait_ge(s_ffn_scale, 1)
                for n, (src, dst, rows) in enumerate(parts):
                    if n:
                        act.wait_ge(s_ffn_sq, n)
                    a(dst, src, ACT.Square, accum_out=sq_parts[0:rows, n:n + 1]).then_inc(s_ffn_sq, 1)

            def ffn_high_parts():
                act.wait_ge(s_ffn_scale, 2)
                a(w_in_hi[:, :, 0:ER].rearrange("p c (e r) -> p e c r", r=R), wd_nat[:, :, :, :],
                  ACT.Copy, scale=s_ffn[:, 0:1])
                a(w_in_hi[:, :, ER:HC], wr_nat[:, :, :], ACT.Copy, scale=s_ffn[:, 0:1])
                a(wu_hi[:, :], wu_nat[:, :], ACT.Copy, scale=s_ffn[:, 1:2])
                a(bu3[:, :], bu_nat[:, :], ACT.Copy, scale=s_ffn[0:Q3, 1:2]).then_inc(s_ffn_hi, 1)

            def step(i, i0, meanwhile=None):
                if some(NP, -1, i0):
                    k = i - 1
                    act.wait_ge(pT_done, k + 1)
                    wait_last(act, y_done, k)
                    a(pT_hi[:, :, :], ps_pT[:, :, :], ACT.Copy).then_inc(pT_hi_done, 1)
                if meanwhile:
                    meanwhile()
                if some(T, -4 - LATE, i0):
                    k = i - 4 - LATE
                    act.wait_ge(wtT_done, k + 1)
                    wait_last(act, o_mm, k)
                    a(wtT_hi[:, :], ps_wT[:, 0, :], ACT.Copy)
                    a(gwT[:, :], ps_wT[0:Q3, 1, :], ACT.Copy).then_inc(wtT_hi_done, 1)
                if some(T, -2 - LATE, i0):
                    k = i - 2 - LATE
                    act.wait_ge(rstd2, k + 1)
                    wait_last(act, h2T_done, k)
                    a(h2[:, :, :], x1[:, col(k), :].rearrange("p o (q c) -> p c (o q)", c=KC),
                      ACT.Identity, bias=mrs[:, 1, col(k)], scale=rs[:, 1, col(k)]).then_inc(normed2, 1)
                if some(T, -3 - LATE, i0):
                    k = i - 3 - LATE
                    act.wait_ge(gap_done, k + 1)
                    a(half_tanh[:, :], gap[:, :], ACT.Tanh, scale=half_inv[:, :]).then_inc(tanh_done, 1)
                if some(NP, 0, i0):
                    k = i
                    act.wait_ge(a_done, k + 1)
                    a(silu[:, :], ps_a[:, :], ACT.Silu, scale=inv_t[:, col(k)]).then_inc(silu_done, 1)
                if some(NP, 1, i0):
                    k = i + 1
                    act.wait_ge(hT_done, k + 1)
                    wait_last(act, a_done, k)
                    a(hT_hi[:, :, :], ps_hT[:, :, :], ACT.Copy).then_inc(hT_hi_done, 1)
                if some(T, -2 - LATE, i0):
                    k = i - 2 - LATE
                    act.wait_ge(h2T_done, k + 1)
                    wait_last(act, hid_mm, k)
                    a(h2T_hi[:, :, :], ps_h2T[:, :, :], ACT.Copy).then_inc(h2T_hi_done, 1)
                if some(NP, 2, i0):
                    k = i + 2
                    tile = (0 if isinstance(k, int) and k == 0 else
                            act.value_load(pair_tile_i[0:1, col(k)], min_val=0, max_val=T - 1))
                    act.wait_ge(rstd1, k + 1 if some(T, 2, i0) else T)
                    wait_last(act, hT_done, k)
                    a(h[:, :], flat(xs[:, col(tile), :]), ACT.Identity,
                      bias=mrs[:, 0, col(tile)], scale=rs[:, 0, col(tile)]).then_inc(normed1, 1)

            act.wait_ge(s_pool, 1)
            a(sq_act[0:1, 0:1], neg_half[0:1, :], ACT.Silu).then_inc(s_sq, 1)
            act.wait_ge(s_sq, 1)
            square_sums(0)
            square_sums(1)
            high_parts(0)
            square_sums(2, range(0, 2))
            step(-2, -2)
            square_sums(2, range(2, KC))
            act.wait_ge(s_places, 1)
            step(-1, -1)
            high_parts(1)
            act.wait_ge(s_gates_in, 16 * 2)
            a(gates[:, :], gates_in[:, :], ACT.Tanh).then_inc(s_gates, 1)
            act.wait_ge(s_tables, 1)
            step(0, 0)
            square_sums(3, range(0, 2))
            step(1, 1, meanwhile=lambda: high_parts(2))
            square_sums(3, range(2, KC))
            ffn_squares()

            def for_pair_2():
                high_parts(3)
                act.wait_ge(s_tables, 2)

            step(2, 2, meanwhile=for_pair_2)
            step(3, 3)
            step(4, 4)
            ffn_high_parts()
            pipeline(act, step, 5, (-1, 0, 1, 2), (2, -2 - LATE, -3 - LATE, -4 - LATE))

        @block.vector
        def _(dve):
            v = nc.vector
            steps = [0]

            def then(ins):
                steps[0] += 1
                ins.then_inc(s_route, 1)
                dve.wait_ge(s_route, steps[0])

            def top_rows(e):
                dve.wait_ge(s_sq, 1 + (e + 1) * KC)
                v.reduce_max(part_sq[:, e:e + 1], row_sq[:, e, :], axis=AX.X).then_inc(s_partsq, 1)

            v.memset(ge[:, 0, :], 1.0)
            v.memset(ge[:, E, :], 0.0)
            v.memset(prev_end[:, 0:1], 0.0)
            v.memset(zeros[:, :], 0.0)
            dve.wait_ge(s_tok, 16)
            for e in range(1, E):
                last = v.tensor_scalar(ge[:, e, :], tok_i[:, :], float(e * PER_EXPERT), None, ALU.is_ge)
            then(last)
            then(v.tensor_tensor(member[:, :, :], ge[:, 0:E, :], ge[:, 1:E + 1, :], ALU.subtract))
            v.reduce_sum(per_row[:, :], member[:, :, :], axis=AX.X).then_inc(s_counts, 1)
            then(v.tensor_tensor_scan(run[:, :], member[:, :, :].rearrange("p e c -> p (e c)"),
                                      zeros[:, :], 0.0, ALU.add, ALU.add))
            then(v.tensor_copy(prev_end[:, 1:E],
                               run[:, :].rearrange("p (e c) -> p e c", c=C)[:, 0:E - 1, C - 1]))
            then(v.reduce_sum(token_e[:, :], ge[:, 1:E, :].rearrange("p e c -> p c e"), axis=AX.X))
            dve.wait_ge(s_const, 1)
            v.tensor_copy(slot_no16[:, :], slot_no[:, :])
            dve.wait_ge(s_rows_mm, 1)
            totals = ps_hid[:, E:2 * E]
            then(v.scalar_tensor_tensor(shift[:, :], ps_hid[:, 0:E], -1.0, prev_end[:, :],
                                        ALU.add, ALU.subtract))
            then(v.tensor_tensor(shift[:, :], shift[:, :], totals, ALU.subtract))
            then(v.tensor_tensor_scan(end_slot[:, :], totals, zeros[:, 0:E], 0.0, ALU.add, ALU.add))
            v.tensor_copy(start_i[:, :], end_slot[:, 0:E - 1])
            then(v.tensor_tensor(shift[:, :], shift[:, :], end_slot[:, :], ALU.add))
            v.tensor_scalar(start_i[:, :], start_i[:, :], 7, None, ALU.logical_shift_right)
            then(v.tensor_tensor(cand[:, :, :], run[:, :].rearrange("p (e c) -> p e c", c=C),
                                 shift[:, :].unsqueeze(2).to_broadcast([P, E, C]), ALU.add))
            v.tensor_copy(start_f[:, :], start_i[:, :])
            then(v.tensor_tensor(cand[:, :, :], cand[:, :, :], member[:, :, :], ALU.mult))
            v.tensor_tensor(first_pair[:, :], start_f[:, :], pair_no[:, 1:E], ALU.add)
            then(v.reduce_sum(slot1[:, :], cand[:, :, :].rearrange("p e c -> p c e"), axis=AX.X))
            then(v.tensor_copy(slot_i[:, :], slot1[:, :]))
            v.tensor_scalar(tile_i[:, :], slot_i[:, :], 7, None, ALU.logical_shift_right)
            then(v.tensor_scalar(in_tile_i[:, :], slot_i[:, :], P - 1, None, ALU.bitwise_and))
            v.tensor_copy(tile_f[:, :], tile_i[:, :])
            then(v.tensor_copy(in_tile_f[:, :], in_tile_i[:, :]))
            v.tensor_copy(in_tile_f32[:, :], in_tile_i[:, :]).then_inc(s_in_tile, 1)

            def hot_slots(c0, c1):
                return v.tensor_tensor(hot_slot[:, c0:c1, :],
                                       in_tile_f[:, c0:c1].unsqueeze(2).to_broadcast([P, c1 - c0, P]),
                                       slot_no16[:, :].unsqueeze(1).to_broadcast([P, c1 - c0, P]),
                                       ALU.is_equal)

            v.tensor_tensor(is_tile[:, :, :], tile_f[:, :].unsqueeze(2).to_broadcast([P, C, T]),
                            pair_no[:, 0:T].unsqueeze(1).to_broadcast([P, C, T]), ALU.is_equal)
            then(hot_slots(0, C // 2))
            v.tensor_tensor(hot_tile[:, :, :], is_tile[:, :, :],
                            row_id1[:, :].unsqueeze(2).to_broadcast([P, C, T]),
                            ALU.mult).then_inc(s_hot, 1)
            top_rows(0)
            hot_slots(C // 2, DVE_HOT).then_inc(s_hot, 1)
            then(v.tensor_tensor(pair_f[:, :], tile_f[:, :], token_e[:, :], ALU.add))

            def top_row(e):
                dve.wait_ge(s_sqT, e + 1)
                v.reduce_max(top_sq[:, e:e + 1], ps_hid[0:1, 0:P], axis=AX.X).then_inc(s_topsq, 1)

            def scale(e):
                dve.wait_ge(s_topall, e + 1)
                then(v.tensor_copy(top_all[:, e:e + 1], ps_hid[:, P:P + 1]))
                then(v.tensor_scalar(half_exp[:, e:e + 1], top_all[:, e:e + 1].bitcast(i32), 24, None,
                                     ALU.logical_shift_right))
                v.tensor_scalar(scale_w[:, e:e + 1], half_exp[:, e:e + 1], -ONE_EXP, SB * ONE_EXP,
                                ALU.mult, ALU.add).then_inc(s_scale, 1)

            def low_parts(e, blocks=None):
                for kc in blocks or range(DVE_LOW[e]):
                    dve.wait_ge(s_whi, e * KC + kc + 1)
                    v.scalar_tensor_tensor(w_lo[:, e, kc, :], w_bank(e, kc), s_w[:, e:e + 1],
                                           w_hi[:, e, kc, :],
                                           ALU.mult, ALU.subtract).then_inc(s_wlo, 1)

            def row_numbers():
                dve.wait_ge(s_rows_mm, 2)
                v.tensor_scalar(rows_of[:, :], ps_hT[:, 0, 0:T], -1.0, None, ALU.add)\
                 .then_inc(s_gather_rows, 1)

            def hot_pairs():
                v.tensor_tensor(hot_pair[:, :, :], pair_f[:, :].unsqueeze(2).to_broadcast([P, C, NP]),
                                pair_no[:, :].unsqueeze(1).to_broadcast([P, C, NP]),
                                ALU.is_equal).then_inc(s_hot_pair, 1)

            def pairs_experts():
                for e in range(E - 1):
                    last = v.tensor_scalar(past[:, e, :], pair_no[:, :], first_pair[:, e:e + 1], None, ALU.is_ge)
                then(last)
                v.reduce_sum(expert_f[:, :], past[:, :, :].rearrange("p e t -> p t e"),
                             axis=AX.X).then_inc(s_expert_f, 1)

            def pair_masks():
                dve.wait_ge(s_expert_f, 1)
                dve.wait_ge(s_rows_mm, 3)
                v.tensor_copy(in_pair[:, :], ps_a[:, 0:NP])
                v.tensor_copy(expert_i[:, :], expert_f[:, :]).then_inc(s_expert, 1)

            def tables(p0, p1):
                cols, seen = slice(p0, p1), min(p1, E)
                then(v.tensor_copy(half_exp_f[:, 0:seen], half_exp[:, 0:seen]))
                for e in range(seen):
                    last = v.tensor_scalar(exp_of[:, e, cols], expert_f[:, cols], float(e),
                                           half_exp_f[:, e:e + 1], ALU.is_equal, ALU.mult)
                then(last)
                then(v.reduce_sum(exp_t[:, cols], exp_of[:, 0:seen, cols].rearrange("p e t -> p t e"),
                                  axis=AX.X))
                v.tensor_scalar(prod_bits[:, cols], exp_t[:, cols], -ONE_EXP, (SB - PK) * ONE_EXP,
                                ALU.mult, ALU.add)
                v.tensor_scalar(inv_bits[:, cols], exp_t[:, cols], ONE_EXP, (254 - SB) * ONE_EXP,
                                ALU.mult, ALU.add).then_inc(s_tables, 1)

            def router_bias():
                dve.wait_ge(s_small, 16 * 8)
                v.tensor_scalar(b_in[:, ER:HC], b_in[:, ER:HC], BONUS, None, ALU.add)\
                 .then_inc(s_ffn_scale, 1)

            def ffn_sums():
                dve.wait_ge(s_ffn_sq, 5)
                then(v.reduce_sum(ffn_parts[:, 0:1], sq_parts[:, 0:3], axis=AX.X))
                then(v.tensor_scalar(ffn_parts[0:1, 0:1], ffn_parts[0:1, 0:1], 1.0, None, ALU.add))
                v.reduce_sum(ffn_parts[:, 1:2], sq_parts[:, 3:5], axis=AX.X).then_inc(s_ffn_part, 1)

            def ffn_scales():
                dve.wait_ge(s_ffn_tot, 1)
                then(v.tensor_copy(ffn_tot[:, :], ps_hid[:, 0:2]))
                then(v.tensor_scalar(ffn_half[:, :], ffn_tot[:, :].bitcast(i32), 24, None,
                                     ALU.logical_shift_right))
                then(v.tensor_scalar(ffn_inv_bits[:, :], ffn_half[:, :], ONE_EXP, (254 - SB) * ONE_EXP,
                                     ALU.mult, ALU.add))
                then(v.tensor_scalar(ffn_bits[:, :], ffn_half[:, :], -ONE_EXP, SB * ONE_EXP,
                                     ALU.mult, ALU.add))
                then(v.tensor_tensor(inv_both[:, :], s_ffn_inv[:, 0:1], s_ffn_inv[:, 1:2], ALU.mult))
                then(v.tensor_tensor(out_coef[:, :], inv_both[:, :], gates[:, 1:2], ALU.mult))
                v.tensor_scalar(half_inv[:, :], s_ffn_inv[:, 0:1], 0.5, None, ALU.mult)\
                 .then_inc(s_ffn_scale, 1)

            def ffn_low_parts():
                v.tensor_scalar(b_s[:, :], b_in[:, :], s_ffn[:, 0:1], None, ALU.mult)
                dve.wait_ge(s_ffn_hi, 1)
                for c in range(KC):
                    v.scalar_tensor_tensor(w_in_lo[:, c, 0:ER].rearrange("p (e r) -> p e r", r=R),
                                           wd_nat[:, :, c, :], s_ffn[:, 0:1],
                                           w_in_hi[:, c, 0:ER].rearrange("p (e r) -> p e r", r=R),
                                           ALU.mult, ALU.subtract)
                v.scalar_tensor_tensor(w_in_lo[:, :, ER:HC], wr_nat[:, :, :], s_ffn[:, 0:1],
                                       w_in_hi[:, :, ER:HC], ALU.mult, ALU.subtract)\
                 .then_inc(s_ffn_w, 1)

            def ffn_out_low_parts():
                v.scalar_tensor_tensor(wu_lo[:, :], wu_nat[:, :], s_ffn[:, 1:2], wu_hi[:, :],
                                       ALU.mult, ALU.subtract)
                low = slice(2 * Q, 2 * Q + EF)
                v.scalar_tensor_tensor(bu3[low, :], bu_nat[low, :], s_ffn[low, 1:2], bu3[low, :],
                                       ALU.mult, ALU.subtract).then_inc(s_ffn_w, 1)

            def gate(n):
                v.memset(gate_cell[:, n:n + 1], 0.0)

            def statistics1(k):
                if isinstance(k, int) and k == 0:
                    dve.wait_ge(s_gather[0], 16)
                else:
                    dve.wait_ge(x_in, k + 1)
                wait_last(dve, aggr1, k)
                gate(0)
                v.bn_stats(st1[:, :], xs[:, col(k), :].rearrange("p o d -> p (o d)")).then_inc(stats1, 1)
                dve.wait_ge(stats1, k + 1)
                wait_last(dve, rstd1, k)
                gate(1)
                v.bn_aggr(mv1[:, :], st1[:, :]).then_inc(aggr1, 1)

            def product(k):
                dve.wait_ge(silu_done, k + 1)
                v.scalar_tensor_tensor(prod[:, :], ps_a[:, :], prod_t[:, col(k)], silu[:, :],
                                       ALU.mult, ALU.mult).then_inc(prod_done, 1)

            def hT_low(k):
                dve.wait_ge(hT_hi_done, k + 1)
                v.tensor_tensor(hT_lo[:, :, :], ps_hT[:, :, :], hT_hi[:, :, :],
                                ALU.subtract).then_inc(hT_lo_done, 1)

            def place(k):
                return (dve.value_load(pair_tile_i[0:1, col(k)], min_val=0, max_val=T - 1),
                        dve.value_load(source_i[0:1, col(k)], min_val=0, max_val=2 * T - 1))

            def add_y(k, tile, source):
                dve.wait_ge(y_done, k + 1)
                wait_last(dve, x1_done, k)
                v.scalar_tensor_tensor(flat(x1[:, col(tile), :]), ps_y[:, :], y_t[:, col(k)],
                                       flat(xs[:, col(source), :]),
                                       ALU.mult, ALU.add).then_inc(x1_done, 1)

            def statistics2(k):
                dve.wait_ge(x1_done, k + 1 + LATE)
                wait_last(dve, aggr2, k)
                gate(2)
                v.bn_stats(st2[:, :], flat(x1[:, col(k), :])).then_inc(stats2, 1)
                dve.wait_ge(stats2, k + 1)
                wait_last(dve, rstd2, k)
                gate(3)
                v.bn_aggr(mv2[:, :], st2[:, :]).then_inc(aggr2, 1)

            def pT_low(k):
                dve.wait_ge(pT_hi_done, k + 1)
                v.tensor_tensor(pT_lo[:, :, :], ps_pT[:, :, :], pT_hi[:, :, :],
                                ALU.subtract).then_inc(pT_lo_done, 1)

            def h2T_low(k):
                dve.wait_ge(h2T_hi_done, k + 1)
                v.tensor_tensor(h2T_lo[:, :, :], ps_h2T[:, :, :], h2T_hi[:, :, :],
                                ALU.subtract).then_inc(h2T_lo_done, 1)

            def add_low_rank(k):
                row = flat(x1[:, col(k), :])
                dve.wait_ge(o_mm, k + 1)
                v.scalar_tensor_tensor(row, ps_o[:, :], out_coef[:, :], row,
                                       ALU.mult, ALU.add).then_inc(out_done, 1)

            def hidden(k):
                dve.wait_ge(hid_mm, k + 1)
                wait_last(dve, weighted_done, k)
                v.tensor_tensor(hid[:, :], ps_hid[:, 0:HC], b_s[:, :], ALU.add).then_inc(hid_done, 1)

            def step(i, i0, meanwhile=None):
                ending = some(NP, -1, i0) and not some(NP, 0, i0)
                draining = not some(NP, -1, i0)
                next_ends = some(NP, 0, i0) and not some(NP, 1, i0)
                if ending:
                    pT_low(i - 1)
                    statistics2(i - 2 - LATE)
                    hidden(i - 3 - LATE)
                if some(T, -3 - LATE, i0):
                    k = i - 3 - LATE
                    dve.wait_ge(hid_done, k + 1)
                    gate(4)
                    v.max(top8[:, :], hid[:, ER:HC]).then_inc(top_done, 1)
                    dve.wait_ge(top_done, k + 1)
                    wait_last(dve, mix_done, k)
                    v.tensor_tensor(gap[:, :], top8[:, 0:1], top8[:, 1:2], ALU.subtract).then_inc(gap_done, 1)
                    v.max_index(arg8[:, :], top8[:, :], hid[:, ER:HC]).then_inc(arg_done, 1)
                if some(T, -4 - LATE, i0):
                    k = i - 4 - LATE
                    dve.wait_ge(wtT_hi_done, k + 1)
                    v.tensor_tensor(wtT_lo[:, :], ps_wT[:, 0, :], wtT_hi[:, :], ALU.subtract)
                    v.tensor_tensor(gwT[Q:Q + EF, :], ps_wT[Q:Q + EF, 1, :], gwT[Q:Q + EF, :],
                                    ALU.subtract).then_inc(wtT_lo_done, 1)
                if some(NP, -1, i0) and not ending:
                    pT_low(i - 1)
                if meanwhile:
                    meanwhile()
                if some(T, 3, i0):
                    statistics1(i + 3)
                if some(T, -2 - LATE, i0) and draining:
                    h2T_low(i - 2 - LATE)
                if ending:
                    add_y(i - 1, *place(i - 1))
                    statistics2(i - 1 - LATE)
                if some(T, -3 - LATE, i0):
                    k = i - 3 - LATE
                    dve.wait_ge(tanh_done, k + 1)
                    dve.wait_ge(mix_done, k + 1)
                    wait_last(dve, wtT_done, k)
                    v.scalar_tensor_tensor(w8[:, :], half_dif[:, :], half_tanh[:, :], half_sum[:, :],
                                           ALU.mult, ALU.add).then_inc(w8_done, 1)
                    dve.wait_ge(w8_done, k + 1)
                    v.scalar_tensor_tensor(
                        weighted[:, :].rearrange("p (e r) -> p e r", r=R),
                        hid[:, 0:ER].rearrange("p (e r) -> p e r", r=R), 0.0,
                        w8[:, :].unsqueeze(2).to_broadcast([P, EF, R]), ALU.max, ALU.mult)
                    v.tensor_scalar(w_rep[:, :, 0:EF], w8[:, :].unsqueeze(1).to_broadcast([P, 3, EF]),
                                    s_ffn[:, 0:1], None, ALU.mult).then_inc(weighted_done, 1)
                if some(NP, 0, i0):
                    product(i)
                if some(NP, 1, i0):
                    hT_low(i + 1)
                if some(T, -2 - LATE, i0) and not draining:
                    h2T_low(i - 2 - LATE)
                if some(T, -4 - LATE, i0) and not draining:
                    add_low_rank(i - 4 - LATE)
                if not ending:
                    if some(NP, -1, i0):
                        add_y(i - 1, *place(i - 1))
                    if some(T, -1 - LATE, i0) and not next_ends:
                        statistics2(i - 1 - LATE)
                if some(T, -2 - LATE, i0) and not next_ends:
                    hidden(i - 2 - LATE)
                if some(T, -4 - LATE, i0) and draining:
                    add_low_rank(i - 4 - LATE)

            top_row(0)
            row_numbers()
            scale(0)
            hot_pairs()
            top_rows(1)
            pairs_experts()
            top_row(1)
            low_parts(0, range(0, 1))
            statistics1(0)
            scale(1)
            low_parts(0, range(1, KC))
            pair_masks()
            statistics1(1)
            top_rows(2)
            hT_low(0)
            top_row(2)
            tables(0, 2)
            statistics1(2)
            low_parts(1)
            scale(2)
            product(0)
            hT_low(1)
            statistics1(3)
            router_bias()
            dve.wait_ge(s_places, 1)
            dve.wait_ge(s_y_t, 1)
            step(1, 1, meanwhile=lambda: low_parts(2))
            top_rows(3)
            top_row(3)
            scale(3)
            tables(2, NP)
            step(2, 2, meanwhile=lambda: low_parts(3))
            ffn_sums()
            dve.wait_ge(s_y_t, 2)
            step(3, 3)
            ffn_scales()
            step(4, 4)
            ffn_low_parts()
            step(5, 5)
            ffn_out_low_parts()
            pipeline(dve, step, 6, (-1, 0, 1), (3, -1 - LATE, -2 - LATE, -3 - LATE, -4 - LATE))


_INS = ['x', 'itok_BxS_13_99985', 'ctx_2048', 'g_xattn', 'g_ffn', 'L0_ffn_Wr', 'L0_ffn_br',
        'L0_ffn_Wd', 'L0_ffn_bd', 'L0_ffn_Wu', 'L0_ffn_bu']
_OUTS = [((4, 512, 512), 'float32')]


def kernel(**inputs):
    import numpy as _np
    import concourse.bacc as _bacc
    from concourse import mybir as _mybir
    from concourse.bass_utils import run_bass_kernel_spmd as _run

    nc = _bacc.Bacc("TRN2", target_bir_lowering=False, num_devices=1)
    arrays, args = {}, []
    for name in _INS:
        a = _np.ascontiguousarray(inputs[name])
        arrays[f"in_{name}_dram"] = a
        args.append(nc.dram_tensor(f"in_{name}_dram", a.shape, _mybir.dt.from_np(a.dtype), kind="ExternalInput").ap())
    for i, (shape, dtype) in enumerate(_OUTS):
        dt = _mybir.dt.from_np(_np.dtype(dtype))
        args.append(nc.dram_tensor(f"out_{i}_dram", shape, dt, kind="ExternalOutput").ap())
    bass_flamingo_gated_kernel(nc, *args)
    r = _run(nc, [arrays], core_ids=[0])
    got = tuple(r.results[0][f"out_{i}_dram"] for i in range(len(_OUTS)))
    return got[0]
```
